# Optimizing a Trainium2 kernel written in Bass

```python
import numpy as np
import jax
import jax.numpy as jnp

def _softmax(x, axis=-1):
    return jax.nn.softmax(x, axis=axis)

def _gelu(x):
    return jax.nn.gelu(x, approximate=True)

def _silu(x):
    return jax.nn.silu(x)

def _sigmoid(x):
    return jax.nn.sigmoid(x)

def _layernorm(x, axis=-1, eps=1e-05):
    m = jnp.mean(x, axis=axis, keepdims=True)
    v = jnp.var(x, axis=axis, keepdims=True)
    return (x - m) / jnp.sqrt(v + eps)

def _scatter_add(tgt, idx, src, axis=0):
    return tgt.at[idx].add(src)

def _segment_sum(src, seg, n):
    return jax.ops.segment_sum(src, seg, n)
kernel_name = 'mk_adaln_ffn_d1_seqx_r8_2e0ff6'

def setup_inputs(seed: int=0):
    np.random.seed(seed)
    _w = jnp.asarray

    def _rec_inputs():
        import jax
        import jax.numpy as jnp
        _rk = jax.random.key(seed)
        x = -0.000125 + 0.9999 * jax.random.normal(jax.random.fold_in(_rk, 1), (128, 32, 512), jnp.float32)
        _lenS = 32 - jax.random.randint(jax.random.fold_in(_rk, 7), (128,), 0, max(1, 32 // 4) + 1, jnp.int32)
        _lenS2 = 32 - jax.random.randint(jax.random.fold_in(_rk, 8), (128,), 0, max(1, 32 // 4) + 1, jnp.int32)
        itok_B_3_7 = jax.random.randint(jax.random.fold_in(_rk, 11), (128,), 3, 8, jnp.int32)
        return (x, itok_B_3_7)
    x, itok_B_3_7 = _rec_inputs()

    def _L0_cond_setup():
        import jax, jax.numpy as jnp
        import numpy as np
        RANK = 16
        ALPHA = 16.0
        SCALING = ALPHA / RANK
        N_ADAPTERS = 8
        IN_F = 512
        OUT_F = 512
        BATCH = 4
        SEQ = 256
        key = jax.random.key(seed)
        kx, ka, kb, ki = jax.random.split(key, 4)
        x = jax.random.normal(kx, (BATCH, SEQ, IN_F), dtype=jnp.float32)
        A = jax.random.normal(ka, (N_ADAPTERS, OUT_F, RANK), dtype=jnp.float32) * 0.02
        B = jax.random.normal(kb, (N_ADAPTERS, RANK, IN_F), dtype=jnp.float32) * 0.02
        adapter_ids = jax.random.randint(ki, (BATCH,), 0, N_ADAPTERS, dtype=jnp.int32)
        return {'x': x, 'A': A, 'B': B, 'adapter_ids': adapter_ids}
    _L0_cond_all = _L0_cond_setup()
    _L0_cond_in = {k: v for k, v in _L0_cond_all.items() if k in ('A', 'B')}
    del _L0_cond_all

    def _L0_ffn_setup():
        import jax, jax.numpy as jnp
        import numpy as np
        D_MODEL = 512
        D_FF = 1376

        def _dequant_matmul(x, w_int, s):
            w = w_int.astype(jnp.float32) * s
            return x @ w.T
        key = jax.random.key(seed)
        ks = jax.random.split(key, 7)
        x = jax.random.normal(ks[0], (4, 256, D_MODEL), dtype=jnp.float32)
        gate_w = jax.random.randint(ks[1], (D_FF, D_MODEL), -128, 128, dtype=jnp.int32)
        up_w = jax.random.randint(ks[2], (D_FF, D_MODEL), -128, 128, dtype=jnp.int32)
        down_w = jax.random.randint(ks[3], (D_MODEL, D_FF), -128, 128, dtype=jnp.int32)
        gate_s = jax.random.uniform(ks[4], (D_FF, 1), dtype=jnp.float32) * 0.01
        up_s = jax.random.uniform(ks[5], (D_FF, 1), dtype=jnp.float32) * 0.01
        down_s = jax.random.uniform(ks[6], (D_MODEL, 1), dtype=jnp.float32) * 0.01
        return {'x': x, 'gate_w': gate_w, 'gate_s': gate_s, 'up_w': up_w, 'up_s': up_s, 'down_w': down_w, 'down_s': down_s}
    _L0_ffn_all = _L0_ffn_setup()
    _L0_ffn_in = {k: v for k, v in _L0_ffn_all.items() if k in ('gate_w', 'gate_s', 'up_w', 'up_s', 'down_w', 'down_s')}
    del _L0_ffn_all
    return {'x': x, 'itok_B_3_7': itok_B_3_7, 'L0_cond_A': _L0_cond_in['A'], 'L0_cond_B': _L0_cond_in['B'], 'L0_ffn_gate_w': _L0_ffn_in['gate_w'], 'L0_ffn_gate_s': _L0_ffn_in['gate_s'], 'L0_ffn_up_w': _L0_ffn_in['up_w'], 'L0_ffn_up_s': _L0_ffn_in['up_s'], 'L0_ffn_down_w': _L0_ffn_in['down_w'], 'L0_ffn_down_s': _L0_ffn_in['down_s']}

def reference(x, itok_B_3_7, L0_cond_A, L0_cond_B, L0_ffn_gate_w, L0_ffn_gate_s, L0_ffn_up_w, L0_ffn_up_s, L0_ffn_down_w, L0_ffn_down_s):
    import jax
    import jax.numpy as jnp

    def _L0_cond_ref(x, A, B, adapter_ids):
        import jax, jax.numpy as jnp
        import numpy as np
        RANK = 16
        ALPHA = 16.0
        SCALING = ALPHA / RANK
        N_ADAPTERS = 8
        IN_F = 512
        OUT_F = 512
        BATCH = 4
        SEQ = 256
        B_sel = B[adapter_ids]
        A_sel = A[adapter_ids]
        Bx = jnp.einsum('bni,bri->bnr', x, B_sel)
        out = jnp.einsum('bnr,bor->bno', Bx, A_sel)
        return out * SCALING

    def _L0_ffn_ref(x, gate_w, gate_s, up_w, up_s, down_w, down_s):
        import jax, jax.numpy as jnp
        import numpy as np
        D_MODEL = 512
        D_FF = 1376

        def _dequant_matmul(x, w_int, s):
            w = w_int.astype(jnp.float32) * s
            return x @ w.T
        batch, seq_len, hidden = x.shape
        x_flat = x.reshape(-1, hidden).astype(jnp.float32)
        gate = _dequant_matmul(x_flat, gate_w, gate_s)
        up = _dequant_matmul(x_flat, up_w, up_s)
        h = jax.nn.silu(gate) * up
        out = _dequant_matmul(h, down_w, down_s)
        return out.astype(x.dtype).reshape(batch, seq_len, hidden)
    x = x + _L0_ffn_ref(_L0_cond_ref(x, L0_cond_A, L0_cond_B, itok_B_3_7), L0_ffn_gate_w, L0_ffn_gate_s, L0_ffn_up_w, L0_ffn_up_s, L0_ffn_down_w, L0_ffn_down_s)
    return x

_drawn_inputs = setup_inputs


def setup_inputs(seed=0):
    import zlib

    import numpy as np

    out = dict(_drawn_inputs(seed))
    spreads = {}
    factors = {}
    for name, (base, spread) in spreads.items():
        noise = np.random.default_rng([zlib.crc32(name.encode()), seed]).standard_normal(out[name].shape)
        drawn = base * np.exp(spread * noise) if base else spread * noise
        out[name] = jnp.asarray(drawn.astype(out[name].dtype))
    for name, factor in factors.items():
        out[name] = (out[name] * factor).astype(out[name].dtype)
    return out
```

```python
from contextlib import ExitStack

import numpy as np

import concourse.bass as bass
from concourse import mybir

F32 = mybir.dt.float32
F32R = mybir.dt.float32r
BF16 = mybir.dt.bfloat16
I32 = mybir.dt.int32
ALU = mybir.AluOpType
ACT = mybir.ActivationFunctionType
AX = mybir.AxisListType

P = 128
NB, TOK, D = 128, 32, 512
NA, R = 8, 16
F = 1376
HALVES, SLOTS = 2, 4
TERMS = 4
PER = P // TOK
NG = NB // PER
DC = D // P
CW = 512
CHUNKS = [(c, min(CW, F - c)) for c in range(0, F, CW)]
NC = len(CHUNKS)
AGW = 2 * F
UNROLL = 4
IOTA, BNUM, IDENT, ADAPTER, WHI, WLO, SELHI = 0, 1, 2, 3, 4, 5, 6
SELLO = SELHI + SLOTS
NCONST = SELLO + SLOTS
NSEL = NCONST - WHI


def blocks_of(width):
    return [(o, min(P, width - o)) for o in range(0, width, P)]


def constants():
    k = np.zeros((P, NCONST * P), np.float32)

    def put(n, m):
        k[:, n * P:(n + 1) * P] = m

    put(IDENT, np.eye(P))
    src = np.arange(P)
    half, slot, rank = src // (SLOTS * R), src // R % SLOTS, src % R
    dst = np.arange(P)
    dhalf, term, drank = dst // (TERMS * R), dst // R % TERMS, dst % R
    same = (half[:, None] == dhalf) & (rank[:, None] == drank)
    put(WHI, same & (term % 2 == 0))
    put(WLO, same & (term % 2 == 1))
    for s in range(SLOTS):
        put(SELHI + s, same & (slot[:, None] == s) & (term // 2 == 0))
        put(SELLO + s, same & (slot[:, None] == s) & (term // 2 == 1))
    put(IOTA, np.arange(P)[None, :])
    put(BNUM, np.arange(P)[:, None])
    put(ADAPTER, (src // R)[:, None])
    return k.astype(mybir.dt.np(BF16))


def reached(engine, sem, count):
    if not isinstance(count, int) or count > 0:
        engine.wait_ge(sem, count)


def over_groups(engine, group):
    for k in range(UNROLL):
        group(0, 0, k)
    with engine.Fori(1, NG // UNROLL - 1) as turn:
        base = engine.snap(turn * UNROLL)
        steps = engine.snap(turn * (UNROLL * NC))
        for k in range(UNROLL):
            group(base, steps, k)
    for k in range(UNROLL):
        group(NG - UNROLL, (NG - UNROLL) * NC, k)


def program(nc, x, ids, lora_a, lora_b, gate_w, gate_s, up_w, up_s, down_w, down_s, consts, out):
    with ExitStack() as ctx:
        def sb(name, shape, dt):
            return ctx.enter_context(nc.sbuf_tensor(name, shape, dt))

        def sem(name):
            return ctx.enter_context(nc.semaphore(name))

        kb = sb("consts_bf", [P, NCONST * P], BF16)
        kf = sb("consts_f32", [P, WHI * P], F32)
        kr = sb("selectors", [P, NSEL * P], F32R)
        ident_bf = kb[:, IDENT * P:(IDENT + 1) * P]
        iota = kf[:, IOTA * P:(IOTA + 1) * P]
        batch_no = kf[:, BNUM * P:(BNUM + 1) * P]
        ident = kf[:, IDENT * P:(IDENT + 1) * P]
        adapter_of_row = kf[:, ADAPTER * P:ADAPTER * P + 1]

        def selector(n):
            return kr[:, (n - WHI) * P:(n - WHI + 1) * P]

        ids_col = sb("ids_col", [P, 1], I32)
        ids_row = sb("ids_row", [P, NB], I32)
        slot_col = sb("slot_col", [P, 1], I32)
        slot_row = sb("slot_row", [P, NB], I32)
        key_col = sb("key_col", [P, 1], F32)
        key_row = sb("key_row", [P, NB], F32)
        before = sb("before", [P, NB], F32)
        place = sb("place", [P, 1], F32)
        ids_f = sb("ids_f", [P, 1], F32)
        permute = sb("permute", [P, NB], F32)
        ids_wide = sb("ids_wide", [P, P], F32)
        order = sb("order", [1, NB], I32)
        sorted_ids = sb("sorted_ids", [1, NB], I32)
        sorted_slots = sb("sorted_slots", [1, NB], I32)
        routes = sb("routes", [1, NG, 2], I32)
        slots_wide = sb("slots_wide", [P, NB], I32)
        slots_past = sb("slots_past", [P, NB], F32)
        slot_mask = sb("slot_mask", [P, SLOTS, NB], F32)
        adapter_mask = sb("adapter_mask", [P, NB], F32)

        a_f = sb("a_f", [P, NA, DC * R], F32)
        a_hi = sb("a_hi", [P, DC, P], F32R)
        a_lo = sb("a_lo", [P, DC, P], F32R)
        b_nat = sb("b_nat", [P, D], F32)
        bt = sb("bt", [P, DC, P], F32)
        scales = sb("scales", [P, AGW], F32)
        down_scale = sb("down_scale", [P, D], F32)
        NBF = 6
        w_bf = sb("w_bf", [P, NBF, 4 * D], BF16)
        gt = sb("gt", [P, 2, DC, CW], F32R)
        ag = sb("ag", [P, 2, CW], F32)
        ag_hi = sb("ag_hi", [P, 2, CW], F32R)
        ag_lo = sb("ag_lo", [P, 2, CW], F32R)
        ag_all = sb("ag_all", [P, SLOTS * AGW], F32R)
        down_t = sb("down_t", [P, len(blocks_of(F)), D], F32R)

        x_in = sb("x_in", [P, UNROLL, D], F32)
        xt = sb("xt", [P, D], F32)
        um = sb("um", [P, P], F32)
        u_hi = sb("u_hi", [P, P], F32R)
        u_lo = sb("u_lo", [P, P], F32R)
        w = sb("w", [P, 2, P], F32R)
        w_slot = sb("w_slot", [P, 2, SLOTS, P], F32R)
        silu = sb("silu", [P, 2, CW], F32)
        h = sb("h", [P, 2, CW], F32)
        h_hi = sb("h_hi", [P, 2, CW], F32R)
        h_lo = sb("h_lo", [P, 2, CW], F32R)
        y = sb("y", [P, 2, D], F32)

        bank = [ctx.enter_context(nc.psum_tensor(f"bank{n}", [P, CW], F32)) for n in range(8)]
        gate_ps, up_ps = [bank[0], bank[2]], [bank[1], bank[3]]
        ht_ps, y_ps = bank[4], [bank[5], bank[7]]
        xt_ps, u_ps, w_ps = bank[6], bank[6][:, 0:P], bank[6][:, P:2 * P]
        wt_ps = [bank[m][:, 0:CW // 2].bitcast(BF16) for m in range(3)]
        ag_ps = bank[3]
        sel_ps = [bank[4], bank[5], bank[7]]
        sort_ps = bank[7]

        table_in = sem("table_in")
        sort_consts_in = sem("sort_consts_in")
        consts_in, ids_in, a_in, b_in = sem("consts_in"), sem("ids_in"), sem("a_in"), sem("b_in")
        scales_in = [sem("gate_scale_in"), sem("up_scale_in"), sem("down_scale_in")]
        NW = 2 * NC + DC
        w_in = [sem(f"w_in{n}") for n in range(NW)]
        sort_step, consts_ready = sem("sort_step"), sem("consts_ready")
        permute_ready, sorted_ready, order_ready = sem("permute_ready"), sem("sorted_ready"), sem("order_ready")
        bt_ready, bt_copied = sem("bt_ready"), sem("bt_copied")
        a_split = sem("a_split")
        wt_ready, wt_copied = sem("wt_ready"), [sem("wt_copied_dve"), sem("wt_copied_act")]
        ag_ready, ag_scaled, ag_hi_ready, ag_lo_ready = sem("ag_ready"), sem("ag_scaled"), sem("ag_hi_ready"), sem("ag_lo_ready")
        sel_ready, sel_copied = sem("sel_ready"), [sem("sel_copied_dve"), sem("sel_copied_act")]
        x_loaded = [sem(f"x_loaded{k}") for k in range(UNROLL)]
        xt_ready, xt_copied = sem("xt_ready"), sem("xt_copied")
        u_ready, um_ready, u_hi_ready, u_split = sem("u_ready"), sem("um_ready"), sem("u_hi_ready"), sem("u_split")
        w_ready, w_copied = sem("w_ready"), sem("w_copied")
        parts_ready = sem("parts_ready")
        gu_ready, silu_ready, h_ready = sem("gu_ready"), sem("silu_ready"), sem("h_ready")
        ht_ready, hi_ready, lo_ready = sem("ht_ready"), sem("hi_ready"), sem("lo_ready")
        down_done, y_scaled, res_ready = sem("down_done"), sem("y_scaled"), sem("res_ready")
        y_stored = [sem("y_stored0"), sem("y_stored1")]

        def w_block(n):
            if n < 2 * NC:
                return D, blocks_of(CHUNKS[n // 2][1])
            return F, [(0, P)]

        def w_parts(n):
            width, tiles = w_block(n)
            full = sum(size == P for _, size in tiles)
            parts = [(P, 0, full * width)]
            if full < len(tiles):
                parts.append((tiles[-1][1], full * width, width))
            return parts

        ROUNDS = range(-1, 2 * NC + 1)
        IN_ROUND = {n: [n + 1] for n in range(-1, 2 * NC - 1)} | {2 * NC - 1: [], 2 * NC: []}
        for n in range(DC):
            IN_ROUND[2 * NC - 3 + min(n, 2)].append(2 * NC + n)
        WT = []
        WT_ROUND, WT_END = {}, {}
        for n in ROUNDS:
            start = len(WT)
            for b in IN_ROUND[n]:
                WT += [(b, q) for q in range(DC if b < 2 * NC else NC)]
                WT_END[b] = len(WT)
            WT_ROUND[n] = range(start, min(start + 3, len(WT))), range(min(start + 3, len(WT)), len(WT))

        DEAL = (0, 1, 1, 0, 1, 1, 0, 1)

        FRONT = 3

        def dealt(m):
            return DEAL[m % len(DEAL)]

        def copied_by(engine_no, count):
            return sum(dealt(m) == engine_no for m in range(count))

        block = ctx.enter_context(nc.Block())

        @block.sync
        def _(sp):
            sp.dma_start(ids_row[:, :], ids.rearrange("(o b) -> o b", o=1).to_broadcast([P, NB])).then_inc(ids_in, 16)
            sp.dma_start(ids_col[:, :], ids.rearrange("(b o) -> b o", o=1)).then_inc(ids_in, 16)
            sp.dma_start(kb[:, 0:WHI * P], consts[:, 0:WHI * P]).then_inc(sort_consts_in, 16)

            sp.dma_start(a_f[:, :, :], lora_a.rearrange("i (p c) r -> p i (c r)", c=DC)).then_inc(a_in, 16)
            sp.dma_start(kb[:, WHI * P:NCONST * P], consts[:, WHI * P:NCONST * P]).then_inc(consts_in, 16)
            sp.dma_start(scales[:, 0:F], gate_s.rearrange("f o -> o f").to_broadcast([P, F])).then_inc(scales_in[0], 16)
            sp.dma_start(scales[:, F:AGW], up_s.rearrange("f o -> o f").to_broadcast([P, F])).then_inc(scales_in[1], 16)
            sp.dma_start(b_nat[:, :], lora_b.rearrange("i r d -> (i r) d")).then_inc(b_in, 16)

            rows_in = x.rearrange("b n d -> (b n) d")
            rows_out = out.rearrange("b n d -> (b n) d")

            held = {use: [sp.alloc_register(f"{use}{j}") for j in range(PER)] for use in ("loaded_batch", "stored_batch")}

            def batches_of(g, use):
                sp.load(held[use], order[0:1, bass.ds(g * PER, PER)])
                return [sp.snap(r, min_val=0, max_val=NB - 1) for r in held[use]]

            def load_x(base, k, ahead):
                slot = (k + ahead) % UNROLL
                batches = batches_of(base + (k + ahead), "loaded_batch")
                if not (isinstance(base, int) and base + k + ahead < UNROLL):
                    sp.wait_ge(res_ready, base + (k + ahead + 1 - UNROLL))
                for j, b in enumerate(batches):
                    sp.dma_start(x_in[j * TOK:(j + 1) * TOK, slot, :], rows_in[bass.ds(b * TOK, TOK), :]).then_inc(x_loaded[slot], 16)

            def store_y(base, k, back):
                g = base + (k - back)
                half = (k - back) % 2
                batches = batches_of(g, "stored_batch")
                sp.wait_ge(res_ready, g + 1)
                for j, b in enumerate(batches):
                    sp.dma_start(rows_out[bass.ds(b * TOK, TOK), :], y[j * TOK:(j + 1) * TOK, half, :]).then_inc(y_stored[half], 16)

            sp.wait_ge(order_ready, 1)
            load_x(0, 0, 0)
            load_x(0, 0, 1)
            sp.dma_start(down_scale[:, :], down_s.rearrange("d o -> o d").to_broadcast([P, D])).then_inc(scales_in[2], 16)

            def group(base, steps, k):
                last = isinstance(base, int) and base + k + 2 >= NG
                if not last:
                    load_x(base, k, 2)
                if not (isinstance(base, int) and base + k == 0):
                    store_y(base, k, 1)

            over_groups(sp, group)
            store_y(NG - UNROLL, UNROLL - 1, 0)
            for half in range(2):
                sp.wait_ge(y_stored[half], 16 * PER * NG // 2)

        @block.gpsimd
        def _(pool):
            for n in range(NW):
                if n >= NBF:
                    pool.wait_ge(wt_ready, WT_END[n - NBF])
                if n < 2 * NC:
                    src = gate_w if n % 2 == 0 else up_w
                    f0 = CHUNKS[n // 2][0]
                    for rows, c0, cols in w_parts(n):
                        r0, tiles = f0 + c0 // D * P, cols // D
                        pool.dma_start(w_bf[0:rows, n % NBF, c0:c0 + cols].rearrange("p (t d) -> p t d", t=tiles),
                                       src[r0:r0 + rows * tiles, :].rearrange("(t p) d -> p t d", t=tiles)).then_inc(w_in[n], 16)
                else:
                    r0 = (n - 2 * NC) * P
                    pool.dma_start(w_bf[:, n % NBF, 0:F], down_w[r0:r0 + P, :]).then_inc(w_in[n], 16)
            def part_slots(base, k, ahead):
                g, par = base + (k + ahead), (k + ahead) % 2
                mask = slot_mask[:, :, bass.ds(g * PER, PER)].unsqueeze(3).to_broadcast([P, SLOTS, PER, TOK])
                pool.wait_ge(w_copied, g + 1)
                nc.gpsimd.tensor_tensor(w_slot[:, par, :, :].rearrange("p s (j t) -> p s j t", j=PER),
                                        w[:, par, :].rearrange("p (j t) -> p j t", j=PER).unsqueeze(1)
                                        .to_broadcast([P, SLOTS, PER, TOK]), mask, ALU.mult).then_inc(parts_ready, 1)

            def add_residual(base, k, back):
                half, slot = (k - back) % 2, (k - back) % UNROLL
                pool.wait_ge(y_scaled, base + (k - back + 1))
                nc.gpsimd.tensor_tensor(y[:, half, :], y[:, half, :], x_in[:, slot, :], ALU.add).then_inc(res_ready, 1)

            pool.wait_ge(order_ready, 2)
            part_slots(0, 0, 0)

            def group(base, steps, k):
                if not (isinstance(base, int) and base + k + 1 == NG):
                    part_slots(base, k, 1)
                if not (isinstance(base, int) and base + k == 0):
                    add_residual(base, k, 1)

            over_groups(pool, group)
            add_residual(NG - UNROLL, UNROLL - 1, 0)

        def wt_copy(engine_no, engine, copy, m):
            n, q = WT[m]
            engine.wait_ge(wt_ready, m + 1)
            src = wt_ps[m % 3]
            if n < 2 * NC:
                width = CHUNKS[n // 2][1]
                if n >= 2:
                    engine.wait_ge(ag_ready, n - 1)
                copy(gt[:, n % 2, q, 0:width], src[:, 0:width]).then_inc(wt_copied[engine_no], 1)
            else:
                c = n - 2 * NC
                tiles = blocks_of(CHUNKS[q][1])
                full = sum(size == P for _, size in tiles)
                k0 = CHUNKS[q][0] // P
                last = copy(down_t[:, k0:k0 + full, c * P:(c + 1) * P],
                            src[:, 0:full * P].rearrange("p (t d) -> p t d", t=full))
                if full < len(tiles):
                    size = tiles[-1][1]
                    last = copy(down_t[0:size, k0 + full, c * P:(c + 1) * P], src[0:size, full * P:(full + 1) * P])
                last.then_inc(wt_copied[engine_no], 1)

        def sel_copy(engine_no, engine, copy, m):
            n, s = divmod(m, SLOTS)
            f0, width = CHUNKS[n // 2]
            at = s * AGW + n % 2 * F + f0
            engine.wait_ge(sel_ready, m + 1)
            copy(ag_all[:, at:at + width], sel_ps[m % 3][:, 0:width]).then_inc(sel_copied[engine_no], 1)

        def prepare(engine_no, engine, copy, ag_stage, ag_low, front):
            for n in ROUNDS:
                front(n)
                early, late = ([m for m in part if dealt(m) == engine_no] for part in WT_ROUND[n])
                for m in early:
                    wt_copy(engine_no, engine, copy, m)
                ag_stage(n)
                for m in late:
                    wt_copy(engine_no, engine, copy, m)
                if 1 <= n <= 2 * NC:
                    for m in range((n - 1) * SLOTS, n * SLOTS):
                        if dealt(m) == engine_no:
                            sel_copy(engine_no, engine, copy, m)
                ag_low(n)

        @block.scalar
        def _(act):
            def copy(dst, src):
                return nc.scalar.activation(dst, src, ACT.Copy)

            act.wait_ge(sort_consts_in, 16)
            nc.scalar.activation(silu[:, 0, 0:1], kb[:, IDENT * P:IDENT * P + 1], ACT.Silu).then_inc(table_in, 1)
            act.wait_ge(table_in, 1)

            def ag_stage(n):
                if 0 <= n < 2 * NC:
                    width = CHUNKS[n // 2][1]
                    act.wait_ge(ag_scaled, n + 1)
                    reached(act, sel_ready, (n - 1) * SLOTS)
                    copy(ag_hi[:, n % 2, 0:width], ag[:, n % 2, 0:width]).then_inc(ag_hi_ready, 1)

            def copy_xt(g):
                act.wait_ge(xt_ready, g + 1)
                reached(act, u_ready, g)
                copy(xt[:, :], xt_ps[:, :]).then_inc(xt_copied, 1)

            def copy_w(g, par):
                act.wait_ge(w_ready, g + 1)
                reached(act, gu_ready, NC * (g - 1))
                reached(act, parts_ready, g - 1)
                copy(w[:, par, :], w_ps).then_inc(w_copied, 1)

            def front(n):
                if n == FRONT - 1:
                    act.wait_ge(bt_ready, 1)
                    copy(bt[:, :, :].rearrange("p c m -> p (c m)"), bank[6][:, :]).then_inc(bt_copied, 1)
                elif n == FRONT:
                    copy_xt(0)
                elif n == FRONT + 2:
                    copy_w(0, 0)

            prepare(1, act, copy, ag_stage, lambda n: None, front)

            def split_hi(s, par):
                act.wait_ge(ht_ready, s + 1)
                reached(act, down_done, s - 1)
                copy(h_hi[:, par, :], ht_ps[:, :]).then_inc(hi_ready, 1)

            def group(base, steps, k):
                g = base + k
                final = isinstance(base, int) and g + 1 == NG
                for c in range(NC):
                    s, par = steps + (k * NC + c), (NC * k + c) % 2
                    if c == 0 and not final:
                        copy_xt(g + 1)
                    if c == 2 and not final:
                        copy_w(g + 1, (k + 1) % 2)
                    width = CHUNKS[c][1]
                    act.wait_ge(gu_ready, s + 1)
                    reached(act, h_ready, s - 1)
                    nc.scalar.activation(silu[:, par, 0:width], gate_ps[par][:, 0:width], ACT.Silu).then_inc(silu_ready, 1)
                    if not (isinstance(s, int) and s == 0):
                        split_hi(s - 1, 1 - par)

            over_groups(act, group)
            split_hi(NG * NC - 1, (NG * NC - 1) % 2)

        @block.vector
        def _(dve):
            steps = [0]

            def then(instruction):
                steps[0] += 1
                instruction.then_inc(sort_step, 1)
                dve.wait_ge(sort_step, steps[0])

            dve.wait_ge(ids_in, 32)
            then(nc.vector.tensor_scalar(slot_row[:, :], ids_row[:, :], SLOTS - 1, None, ALU.bitwise_and))
            then(nc.vector.tensor_scalar(slot_col[:, :], ids_col[:, :], SLOTS - 1, None, ALU.bitwise_and))
            dve.wait_ge(sort_consts_in, 16)
            then(nc.vector.tensor_copy(kf[:, :], kb[:, 0:WHI * P]))
            then(nc.vector.scalar_tensor_tensor(key_row[:, :], slot_row[:, :], float(NB), iota, ALU.mult, ALU.add))
            then(nc.vector.scalar_tensor_tensor(key_col[:, :], slot_col[:, :], float(NB), batch_no[:, 0:1], ALU.mult, ALU.add))
            then(nc.vector.tensor_copy(ids_f[:, :], ids_col[:, :]))
            then(nc.vector.tensor_scalar(before[:, :], key_row[:, :], key_col[:, 0:1], None, ALU.is_lt))
            then(nc.vector.tensor_reduce(place[:, :], before[:, :], AX.X, ALU.add))
            nc.vector.tensor_scalar(ids_wide[:, :], iota, 0.0, ids_f[:, 0:1], ALU.mult, ALU.add)
            nc.vector.tensor_scalar(permute[:, :], iota, place[:, 0:1], None, ALU.is_equal).then_inc(permute_ready, 1)
            def finish_sort():
                dve.wait_ge(sorted_ready, 1)
                nc.vector.tensor_copy(order[:, :], sort_ps[0:1, 0:NB]).then_inc(order_ready, 1)
                then(nc.vector.tensor_copy(sorted_ids[:, :], sort_ps[0:1, NB:2 * NB]))
                then(nc.vector.tensor_scalar(sorted_slots[:, :], sorted_ids[:, :], SLOTS - 1, None, ALU.bitwise_and))
                by_group = sorted_slots[:, :].rearrange("o (g j) -> o g j", j=PER)
                nc.vector.tensor_copy(routes[:, :, 0], by_group[:, :, 0])
                nc.vector.tensor_tensor(routes[:, :, 1], by_group[:, :, PER - 1], by_group[:, :, 0], ALU.subtract)
                nc.vector.tensor_scalar(adapter_mask[:, :], sort_ps[:, NB:2 * NB], adapter_of_row, None, ALU.is_equal)
                then(nc.vector.tensor_copy(slots_wide[:, :], sort_ps[:, NB:2 * NB]))
                then(nc.vector.tensor_scalar(slots_wide[:, :], slots_wide[:, :], SLOTS - 1, None, ALU.bitwise_and))
                wide = slots_wide[:, :].rearrange("p (g j) -> p g j", j=PER)
                then(nc.vector.tensor_tensor(slots_past[:, :].rearrange("p (g j) -> p g j", j=PER), wide,
                                             wide[:, :, 0:1].to_broadcast([P, NG, PER]), ALU.subtract))
                for n in range(SLOTS):
                    last = nc.vector.tensor_scalar(slot_mask[:, n, :], slots_past[:, :], float(n), None, ALU.is_equal)
                last.then_inc(order_ready, 1)

            dve.wait_ge(a_in, 16)
            a_by_chunk = a_f[:, :, :].rearrange("p i (c r) -> p c i r", c=DC)
            hi, lo = (a[:, :, :].rearrange("p c (i r) -> p c i r", i=NA) for a in (a_hi, a_lo))
            then(nc.vector.tensor_copy(hi, a_by_chunk))
            nc.vector.tensor_tensor(lo, a_by_chunk, hi, ALU.subtract).then_inc(a_split, 1)
            dve.wait_ge(consts_in, 16)
            nc.vector.tensor_copy(kr[:, :], kb[:, WHI * P:NCONST * P]).then_inc(consts_ready, 1)

            def ag_stage(n):
                if n == 0:
                    dve.wait_ge(scales_in[0], 16)
                if n == 1:
                    dve.wait_ge(scales_in[1], 16)
                if 0 <= n < 2 * NC:
                    f0, width = CHUNKS[n // 2]
                    at = n % 2 * F + f0
                    dve.wait_ge(ag_ready, n + 1)
                    reached(dve, ag_lo_ready, n - 1)
                    nc.vector.tensor_tensor(ag[:, n % 2, 0:width], ag_ps[:, 0:width], scales[:, at:at + width],
                                            ALU.mult).then_inc(ag_scaled, 1)

            def ag_low(n):
                if not 0 <= n < 2 * NC:
                    return
                par, width = n % 2, CHUNKS[n // 2][1]
                dve.wait_ge(ag_hi_ready, n + 1)
                nc.vector.tensor_tensor(ag_lo[:, par, 0:width], ag[:, par, 0:width], ag_hi[:, par, 0:width],
                                        ALU.subtract).then_inc(ag_lo_ready, 1)

            def split_u(base, k, ahead):
                g = base + (k + ahead)
                mask = adapter_mask[:, bass.ds(g * PER, PER)].unsqueeze(2).to_broadcast([P, PER, TOK])
                src = u_ps.rearrange("p (j t) -> p j t", j=PER)
                dve.wait_ge(u_ready, g + 1)
                reached(dve, u_split, g)
                nc.vector.tensor_tensor(um[:, :].rearrange("p (j t) -> p j t", j=PER), src, mask, ALU.mult).then_inc(um_ready, 1)
                reached(dve, w_ready, g)
                dve.wait_ge(um_ready, g + 1)
                nc.vector.tensor_copy(u_hi[:, :], um[:, :]).then_inc(u_hi_ready, 1)
                dve.wait_ge(u_hi_ready, g + 1)
                nc.vector.tensor_tensor(u_lo[:, :], um[:, :], u_hi[:, :], ALU.subtract).then_inc(u_split, 1)

            def front(n):
                if n == 0:
                    finish_sort()
                elif n == FRONT + 1:
                    split_u(0, 0, 0)

            prepare(0, dve, nc.vector.tensor_copy, ag_stage, ag_low, front)

            dve.wait_ge(scales_in[2], 16)

            def split_lo(s, par):
                dve.wait_ge(hi_ready, s + 1)
                nc.vector.tensor_tensor(h_lo[:, par, :], ht_ps[:, :], h_hi[:, par, :], ALU.subtract).then_inc(lo_ready, 1)

            def scale_y(base, k, back):
                g, half = base + (k - back), (k - back) % 2
                dve.wait_ge(down_done, NC * (g + 1))
                if not isinstance(g, int) or g >= 2:
                    dve.wait_ge(y_stored[half], 8 * PER * (base + (k - back - half)))
                nc.vector.tensor_tensor(y[:, half, :], y_ps[half][:, :], down_scale[:, :], ALU.mult).then_inc(y_scaled, 1)

            def group(base, steps, k):
                g = base + k
                final = isinstance(base, int) and g + 1 == NG
                for c in range(NC):
                    s, par = steps + (k * NC + c), (NC * k + c) % 2
                    if c == 1 and not final:
                        split_u(base, k, 1)
                    if c == 2 and not (isinstance(g, int) and g == 0):
                        scale_y(base, k, 1)
                    width = CHUNKS[c][1]
                    dve.wait_ge(silu_ready, s + 1)
                    reached(dve, ht_ready, s - 1)
                    nc.vector.tensor_tensor(h[:, par, 0:width], silu[:, par, 0:width], up_ps[par][:, 0:width],
                                            ALU.mult).then_inc(h_ready, 1)
                    if not (isinstance(s, int) and s == 0):
                        split_lo(s - 1, 1 - par)

            over_groups(dve, group)
            split_lo(NG * NC - 1, (NG * NC - 1) % 2)
            scale_y(NG - UNROLL, UNROLL - 1, 0)

        @block.tensor
        def _(pe):
            def sort_products():
                pe.wait_ge(permute_ready, 1)
                nc.tensor.matmul(sort_ps[:, 0:NB], batch_no, permute[:, :], start=True, stop=True)
                nc.tensor.matmul(sort_ps[:, NB:2 * NB], ids_wide[:, :], permute[:, :], start=True, stop=True)\
                  .then_inc(sorted_ready, 1)

            def wt_transposes(m):
                n, q = WT[m]
                if q == 0:
                    pe.wait_ge(w_in[n], 16 * len(w_parts(n)))
                if m >= 3:
                    pe.wait_ge(wt_copied[dealt(m - 3)], copied_by(dealt(m - 3), m - 2))
                dst = wt_ps[m % 3]
                if n < 2 * NC:
                    for t, (o, size) in enumerate(blocks_of(CHUNKS[n // 2][1])):
                        rows = w_bf[0:size, n % NBF, t * D:(t + 1) * D].rearrange("f (p c) -> f c p", c=DC)
                        last = nc.tensor.transpose(dst[:, o:o + size], rows[:, q, :], ident_bf[0:size, 0:size])
                else:
                    for t, (o, size) in enumerate(blocks_of(CHUNKS[q][1])):
                        at = CHUNKS[q][0] + o
                        last = nc.tensor.transpose(dst[0:size, t * P:(t + 1) * P], w_bf[:, n % NBF, at:at + size],
                                                   ident_bf)
                last.then_inc(wt_ready, 1)

            def ag_products(n):
                if n == 0:
                    pe.wait_ge(a_split, 1)
                width = CHUNKS[n // 2][1]
                reached(pe, ag_scaled, n)
                for e in range(2):
                    pe.wait_ge(wt_copied[e], copied_by(e, WT_END[n]))
                for q in range(DC):
                    for part in (a_lo, a_hi):
                        last = nc.tensor.matmul(ag_ps[:, 0:width], part[:, q, :], gt[:, n % 2, q, 0:width],
                                                start=(q == 0 and part is a_lo), stop=(q == DC - 1 and part is a_hi))
                last.then_inc(ag_ready, 1)

            def spread(n):
                width = CHUNKS[n // 2][1]
                if n == 0:
                    pe.wait_ge(consts_ready, 1)
                pe.wait_ge(ag_lo_ready, n + 1)
                for s in range(SLOTS):
                    m = n * SLOTS + s
                    if m >= 3:
                        pe.wait_ge(sel_copied[dealt(m - 3)], copied_by(dealt(m - 3), m - 2))
                    elif m == 0:
                        pe.wait_ge(order_ready, 2)
                    nc.tensor.matmul(sel_ps[m % 3][:, 0:width], selector(SELHI + s), ag_hi[:, n % 2, 0:width], start=True, stop=False)
                    nc.tensor.matmul(sel_ps[m % 3][:, 0:width], selector(SELLO + s), ag_lo[:, n % 2, 0:width],
                                     start=False, stop=True).then_inc(sel_ready, 1)

            def transpose_x(base, k, ahead):
                g, slot = base + (k + ahead), (k + ahead) % UNROLL
                pe.wait_ge(x_loaded[slot], 16 * (base + (k + ahead - slot)) + 16 * PER)
                for c in range(DC):
                    last = nc.tensor.transpose(xt_ps[:, c * P:(c + 1) * P], x_in[:, slot, c * P:(c + 1) * P], ident)
                last.then_inc(xt_ready, 1)

            def down_ranks(g):
                pe.wait_ge(xt_copied, g + 1)
                for c in range(DC):
                    last = nc.tensor.matmul(u_ps, bt[:, c, :], xt[:, c * P:(c + 1) * P], start=(c == 0), stop=(c == DC - 1))
                last.then_inc(u_ready, 1)

            def spread_u(g):
                if isinstance(g, int) and g == 0:
                    pe.wait_ge(consts_ready, 1)
                pe.wait_ge(u_split, g + 1)
                nc.tensor.matmul(w_ps, selector(WHI), u_hi[:, :], start=True, stop=False)
                nc.tensor.matmul(w_ps, selector(WLO), u_lo[:, :], start=False, stop=True).then_inc(w_ready, 1)

            def front(n):
                if n == -1:
                    pe.wait_ge(sort_consts_in, 16)
                if n == FRONT - 1:
                    pe.wait_ge(b_in, 16)
                    for c in range(DC):
                        last = nc.tensor.transpose(bank[6][:, c * P:(c + 1) * P], b_nat[:, c * P:(c + 1) * P], ident)
                    last.then_inc(bt_ready, 1)
                elif n == FRONT:
                    pe.wait_ge(bt_copied, 1)
                    transpose_x(0, 0, 0)
                elif n == FRONT + 1:
                    down_ranks(0)
                elif n == FRONT + 2:
                    spread_u(0)

            for n in ROUNDS:
                front(n)
                for m in WT_ROUND[n][0]:
                    wt_transposes(m)
                if n == -1:
                    sort_products()
                if 0 <= n < 2 * NC:
                    ag_products(n)
                for m in WT_ROUND[n][1]:
                    wt_transposes(m)
                if 1 <= n <= 2 * NC:
                    spread(n - 1)

            for e in range(2):
                pe.wait_ge(wt_copied[e], copied_by(e, len(WT)))

            def spread_in_place(c):
                for e in range(2):
                    pe.wait_ge(sel_copied[e], copied_by(e, 2 * (c + 1) * SLOTS))

            def gate_up(base, s, k, c, route):
                g, par = base + k, (NC * k + c) % 2
                f0, width = CHUNKS[c]
                first_slot, meets = route

                def products(lhs, slot, start, stop):
                    for kind, dst in ((0, gate_ps[par]), (1, up_ps[par])):
                        at = slot * AGW + (kind * F + f0)
                        last = nc.tensor.matmul(dst[:, 0:width], lhs, ag_all[:, bass.ds(at, width)], start=start, stop=stop)
                    if stop:
                        last.then_inc(gu_ready, 1)

                with pe.If(meets == 0):
                    if c == 0:
                        pe.wait_ge(w_copied, g + 1)
                    products(w[:, k % 2, :], first_slot, True, True)
                with pe.Else():
                    if c == 0:
                        pe.wait_ge(parts_ready, g + 1)
                    with pe.If(meets == 1):
                        for n in range(2):
                            products(w_slot[:, k % 2, n, :], (first_slot + n) % SLOTS, n == 0, n == 1)
                    with pe.Else():
                        for n in range(SLOTS):
                            products(w_slot[:, k % 2, n, :], (first_slot + n) % SLOTS, n == 0, n == SLOTS - 1)

            routes_held = [[pe.alloc_register(f"route{par}{n}") for n in range(2)] for par in range(2)]

            def load_route(g, par):
                pe.load(routes_held[par], routes[0:1, bass.ds(g, 1), :])

            load_route(0, 0)

            def transpose_h(s, par, c):
                pe.wait_ge(h_ready, s + 1)
                reached(pe, lo_ready, s)
                for o, size in blocks_of(CHUNKS[c][1]):
                    last = nc.tensor.transpose(ht_ps[0:size, o:o + P], h[:, par, o:o + size], ident)
                last.then_inc(ht_ready, 1)

            def down(g, half, s, par, c):
                if c == 0:
                    reached(pe, y_scaled, g - 1)
                tiles = blocks_of(CHUNKS[c][1])
                for o, size in tiles:
                    n = (CHUNKS[c][0] + o) // P
                    for part in (h_lo, h_hi):
                        last = nc.tensor.matmul(y_ps[half][:, :], part[0:size, par, o:o + P], down_t[0:size, n, :],
                                                start=(n == 0 and part is h_lo),
                                                stop=(c == NC - 1 and o == tiles[-1][0] and part is h_hi))
                last.then_inc(down_done, 1)

            def group(base, steps, k):
                g = base + k
                final = isinstance(base, int) and g + 1 == NG
                first = isinstance(base, int) and g == 0
                route = [pe.snap(r, min_val=0, max_val=SLOTS - 1) for r in routes_held[k % 2]]
                for c in range(NC):
                    s, par = steps + (k * NC + c), (NC * k + c) % 2
                    if c == 1 and not final:
                        down_ranks(g + 1)
                    if c == 2 and not final:
                        spread_u(g + 1)
                    if first:
                        spread_in_place(0 if c == 0 else NC - 1)
                    gate_up(base, s, k, c, route)
                    if c == 0 and not final:
                        transpose_x(base, k, 1)
                    if c == 1 and not final:
                        load_route(g + 1, (k + 1) % 2)
                    if not (first and c == 0):
                        transpose_h(s - 1, 1 - par, (c - 1) % NC)
                    if not (first and c < 2):
                        down(g if c == 2 else g - 1, (k + (c == 2) + 1) % 2, s - 2, par, (c - 2) % NC)

            over_groups(pe, group)
            S = NG * NC
            transpose_h(S - 1, (S - 1) % 2, NC - 1)
            down(NG - 1, (NG - 1) % 2, S - 2, S % 2, NC - 2)
            pe.wait_ge(lo_ready, S)
            down(NG - 1, (NG - 1) % 2, S - 1, (S - 1) % 2, NC - 1)


def kernel(x, itok_B_3_7, L0_cond_A, L0_cond_B, L0_ffn_gate_w, L0_ffn_gate_s, L0_ffn_up_w, L0_ffn_up_s,
           L0_ffn_down_w, L0_ffn_down_s):
    import concourse.bacc as bacc
    from concourse.bass_utils import run_bass_kernel_spmd

    arrays = {"x_in_dram": x, "ids_dram": itok_B_3_7, "lora_a_dram": L0_cond_A, "lora_b_dram": L0_cond_B,
              "gate_w_dram": L0_ffn_gate_w, "gate_s_dram": L0_ffn_gate_s, "up_w_dram": L0_ffn_up_w,
              "up_s_dram": L0_ffn_up_s, "down_w_dram": L0_ffn_down_w, "down_s_dram": L0_ffn_down_s,
              "consts_dram": constants()}
    arrays = {name: np.ascontiguousarray(a) for name, a in arrays.items()}
    nc = bacc.Bacc("TRN2", target_bir_lowering=False, num_devices=1)
    aps = [nc.dram_tensor(name, a.shape, mybir.dt.from_np(a.dtype), kind="ExternalInput").ap() for name, a in arrays.items()]
    out = nc.dram_tensor("out_dram", (NB, TOK, D), F32, kind="ExternalOutput").ap()
    program(nc, *aps, out)
    r = run_bass_kernel_spmd(nc, [arrays], core_ids=[0])
    return r.results[0]["out_dram"]
```

```python
from contextlib import ExitStack

import numpy as np

import concourse.bass as bass
from concourse import mybir

F32 = mybir.dt.float32
F32R = mybir.dt.float32r
BF16 = mybir.dt.bfloat16
I32 = mybir.dt.int32
ALU = mybir.AluOpType
ACT = mybir.ActivationFunctionType
AX = mybir.AxisListType

P = 128
NB, TOK, D = 128, 32, 512
NA, R = 8, 16
F = 1376
HALVES, SLOTS = 2, 4
TERMS = 4
PER = P // TOK
NG = NB // PER
DC = D // P
CW = 512
CHUNKS = [(c, min(CW, F - c)) for c in range(0, F, CW)]
NC = len(CHUNKS)
AGW = 2 * F
WARMUP = 10
UNROLL = 4
IOTA, BNUM, IDENT, ADAPTER, WHI, WLO, SELHI, SELLO = 0, 1, 2, 3, 4, 5, 6, 7
NCONST = SELLO + 1
NSEL = NCONST - WHI


def blocks_of(width):
    return [(o, min(P, width - o)) for o in range(0, width, P)]


def constants():
    k = np.zeros((P, NCONST * P), np.float32)

    def put(n, m):
        k[:, n * P:(n + 1) * P] = m

    put(IDENT, np.eye(P))
    src = np.arange(P)
    half, slot, rank = src // (SLOTS * R), src // R % SLOTS, src % R
    dst = np.arange(P)
    dhalf, term, drank = dst // (TERMS * R), dst // R % TERMS, dst % R
    same = (half[:, None] == dhalf) & (rank[:, None] == drank)
    put(WHI, same & (term % 2 == 0))
    put(WLO, same & (term % 2 == 1))
    put(SELHI, same & (slot[:, None] == 0) & (term // 2 == 0))
    put(SELLO, same & (slot[:, None] == 0) & (term // 2 == 1))
    put(IOTA, np.arange(P)[None, :])
    put(BNUM, np.arange(P)[:, None])
    put(ADAPTER, (src // R)[:, None])
    return k.astype(mybir.dt.np(BF16))


def reached(engine, sem, count):
    if not isinstance(count, int) or count > 0:
        engine.wait_ge(sem, count)


def over_groups(engine, group):
    for k in range(UNROLL):
        group(0, 0, k)
    with engine.Fori(1, NG // UNROLL - 1) as turn:
        base = engine.snap(turn * UNROLL)
        steps = engine.snap(turn * (UNROLL * NC))
        for k in range(UNROLL):
            group(base, steps, k)
    for k in range(UNROLL):
        group(NG - UNROLL, (NG - UNROLL) * NC, k)


def program(nc, x, ids, lora_a, lora_b, gate_w, gate_s, up_w, up_s, down_w, down_s, consts, out):
    with ExitStack() as ctx:
        def sb(name, shape, dt):
            return ctx.enter_context(nc.sbuf_tensor(name, shape, dt))

        def sem(name):
            return ctx.enter_context(nc.semaphore(name))

        kb = sb("consts_bf", [P, NCONST * P], BF16)
        kf = sb("consts_f32", [P, WHI * P], F32)
        kr = sb("selectors", [P, NSEL * P], F32R)
        ident_bf = kb[:, IDENT * P:(IDENT + 1) * P]
        iota = kf[:, IOTA * P:(IOTA + 1) * P]
        batch_no = kf[:, BNUM * P:(BNUM + 1) * P]
        ident = kf[:, IDENT * P:(IDENT + 1) * P]
        adapter_of_row = kf[:, ADAPTER * P:ADAPTER * P + 1]

        def selector(n):
            return kr[:, (n - WHI) * P:(n - WHI + 1) * P]

        ids_col = sb("ids_col", [P, 1], I32)
        ids_row = sb("ids_row", [P, NB], I32)
        slot_col = sb("slot_col", [P, 1], I32)
        slot_row = sb("slot_row", [P, NB], I32)
        key_col = sb("key_col", [P, 1], F32)
        key_row = sb("key_row", [P, NB], F32)
        before = sb("before", [P, NB], F32)
        place = sb("place", [P, 1], F32)
        ids_f = sb("ids_f", [P, 1], F32)
        permute = sb("permute", [P, NB], F32)
        ids_wide = sb("ids_wide", [P, P], F32)
        order = sb("order", [1, NB], I32)
        sorted_ids = sb("sorted_ids", [P, NB], I32)
        routes = sb("routes", [1, NG, 2], I32)
        slots_wide = sb("slots_wide", [P, NB], I32)
        slots_past = sb("slots_past", [P, NB], F32)
        slot_mask = sb("slot_mask", [P, SLOTS, NB], F32)
        adapter_mask = sb("adapter_mask", [P, NB], F32)

        a_f = sb("a_f", [P, NA, DC * R], F32)
        a_hi = sb("a_hi", [P, DC, P], F32R)
        a_lo = sb("a_lo", [P, DC, P], F32R)
        b_nat = sb("b_nat", [P, D], F32)
        bt = sb("bt", [P, DC, P], F32)
        scales = sb("scales", [P, AGW], F32)
        down_scale = sb("down_scale", [P, D], F32)
        NBF = 6
        w_bf = sb("w_bf", [P, NBF, 4 * D], BF16)
        gt = sb("gt", [P, 2, DC, CW], F32R)
        ag = sb("ag", [P, 2, CW], F32)
        ag_hi = sb("ag_hi", [P, AGW], F32R)
        ag_lo = sb("ag_lo", [P, AGW], F32R)
        ag_all = sb("ag_all", [P, SLOTS * AGW], F32R)
        down_t = sb("down_t", [P, len(blocks_of(F)), D], F32R)

        x_in = sb("x_in", [P, UNROLL, D], F32)
        xt = sb("xt", [P, D], F32)
        um = sb("um", [P, P], F32)
        u_hi = sb("u_hi", [P, P], F32R)
        u_lo = sb("u_lo", [P, P], F32R)
        w = sb("w", [P, 2, P], F32R)
        w_slot = sb("w_slot", [P, 2, SLOTS, P], F32R)
        silu = sb("silu", [P, 2, CW], F32)
        h = sb("h", [P, 2, CW], F32)
        h_hi = sb("h_hi", [P, 2, CW], F32R)
        h_lo = sb("h_lo", [P, 2, CW], F32R)
        y = sb("y", [P, 2, D], F32)

        bank = [ctx.enter_context(nc.psum_tensor(f"bank{n}", [P, CW], F32)) for n in range(8)]
        gate_ps, up_ps = [bank[0], bank[2]], [bank[1], bank[3]]
        ht_ps, y_ps = bank[4], [bank[5], bank[7]]
        xt_ps, u_ps, w_ps = bank[6], bank[6][:, 0:P], bank[6][:, P:2 * P]
        wt_ps = [bank[m][:, 0:CW // 2].bitcast(BF16) for m in (0, 1, 2, 4)]
        ag_ps = bank[3]
        sel_ps = [bank[5], bank[7]]
        sort_ps = bank[7]

        warm = sb("warm", [P, CW], BF16)
        warm_ready = sem("warm_ready")
        table_in = sem("table_in")
        sort_consts_in = sem("sort_consts_in")
        consts_in, ids_in, a_in, b_in = sem("consts_in"), sem("ids_in"), sem("a_in"), sem("b_in")
        scales_in, down_scale_in = [sem(f"scales_in{n}") for n in range(2 * NC)], sem("down_scale_in")
        NW = 2 * NC + DC
        w_in = [sem(f"w_in{n}") for n in range(NW)]
        sort_step, consts_ready = sem("sort_step"), sem("consts_ready")
        permute_ready, sorted_ready, order_ready = sem("permute_ready"), sem("sorted_ready"), sem("order_ready")
        bt_ready, bt_copied = sem("bt_ready"), sem("bt_copied")
        a_split = sem("a_split")
        wt_ready, wt_copied = sem("wt_ready"), [sem("wt_copied_dve"), sem("wt_copied_act")]
        ag_ready, ag_scaled, ag_hi_ready, ag_lo_ready = sem("ag_ready"), sem("ag_scaled"), sem("ag_hi_ready"), sem("ag_lo_ready")
        sel_ready, sel_copied = sem("sel_ready"), [sem("sel_copied_dve"), sem("sel_copied_act")]
        slots_in = sem("slots_in")
        x_loaded = [sem(f"x_loaded{k}") for k in range(UNROLL)]
        xt_ready, xt_copied = sem("xt_ready"), sem("xt_copied")
        u_ready, um_ready, u_hi_ready, u_split = sem("u_ready"), sem("um_ready"), sem("u_hi_ready"), sem("u_split")
        w_ready, w_copied = sem("w_ready"), sem("w_copied")
        parts_ready = sem("parts_ready")
        gu_ready, silu_ready, h_ready = sem("gu_ready"), sem("silu_ready"), sem("h_ready")
        ht_ready, hi_ready, lo_ready = sem("ht_ready"), sem("hi_ready"), sem("lo_ready")
        down_done, y_scaled, res_ready = sem("down_done"), sem("y_scaled"), sem("res_ready")
        last_res_ready = sem("last_res_ready")
        y_stored = [sem("y_stored0"), sem("y_stored1")]

        SLOT_DMAS = (SLOTS - 1) * HALVES * TERMS

        def ag_columns(n):
            f0, width = CHUNKS[n // 2]
            return slice(n % 2 * F + f0, n % 2 * F + f0 + width)

        def w_block(n):
            if n < 2 * NC:
                return D, blocks_of(CHUNKS[n // 2][1])
            return F, [(0, P)]

        def w_parts(n):
            width, tiles = w_block(n)
            full = sum(size == P for _, size in tiles)
            parts = [(P, 0, full * width)]
            if full < len(tiles):
                parts.append((tiles[-1][1], full * width, width))
            return parts

        ROUNDS = range(-1, 2 * NC)
        IN_ROUND = {n: [n + 1] for n in range(-1, 2 * NC - 1)} | {2 * NC - 1: []}
        for n in range(DC):
            IN_ROUND[2 * NC - 3 + min(n, 2)].append(2 * NC + n)
        WT_RING = len(wt_ps)
        WT = []
        WT_ROUND, WT_END = {}, {}
        for n in ROUNDS:
            start = len(WT)
            for b in IN_ROUND[n]:
                WT += [(b, q) for q in range(DC if b < 2 * NC else NC)]
                WT_END[b] = len(WT)
            WT_ROUND[n] = range(start, min(start + WT_RING, len(WT))), range(min(start + WT_RING, len(WT)), len(WT))

        DEAL = (1, 1, 1, 1) + (0, 1, 1, 0, 1, 1, 0, 1) * 4

        SEL_DEAL = (0, 1, 0, 1, 1, 0)

        FRONT = 3

        def dealt(m):
            return DEAL[m]

        def copied_by(engine_no, count):
            return sum(dealt(m) == engine_no for m in range(count))

        def sel_copied_by(engine_no, count):
            return sum(e == engine_no for e in SEL_DEAL[:count])

        block = ctx.enter_context(nc.Block())

        @block.sync
        def _(sp):
            sp.dma_start(ids_row[:, :], ids.rearrange("(o b) -> o b", o=1).to_broadcast([P, NB])).then_inc(ids_in, 16)
            sp.dma_start(ids_col[:, :], ids.rearrange("(b o) -> b o", o=1)).then_inc(ids_in, 16)
            sp.dma_start(kb[:, 0:WHI * P], consts[:, 0:WHI * P]).then_inc(sort_consts_in, 16)

            sp.dma_start(a_f[:, :, :], lora_a.rearrange("i (p c) r -> p i (c r)", c=DC)).then_inc(a_in, 16)
            sp.dma_start(kb[:, WHI * P:NCONST * P], consts[:, WHI * P:NCONST * P]).then_inc(consts_in, 16)

            def load_scales(n):
                (f0, width), src = CHUNKS[n // 2], gate_s if n % 2 == 0 else up_s
                sp.dma_start(scales[:, ag_columns(n)], src[f0:f0 + width, :].rearrange("f o -> o f").to_broadcast([P, width]))\
                  .then_inc(scales_in[n], 16)

            load_scales(0)

            rows_in = x.rearrange("b n d -> (b n) d")
            rows_out = out.rearrange("b n d -> (b n) d")

            held = {use: [sp.alloc_register(f"{use}{j}") for j in range(PER)] for use in ("loaded_batch", "stored_batch")}

            def batches_of(g, use):
                sp.load(held[use], order[0:1, bass.ds(g * PER, PER)])
                return [sp.snap(r, min_val=0, max_val=NB - 1) for r in held[use]]

            def load_x(base, k, ahead):
                slot = (k + ahead) % UNROLL
                batches = batches_of(base + (k + ahead), "loaded_batch")
                if not (isinstance(base, int) and base + k + ahead < UNROLL):
                    sp.wait_ge(res_ready, base + (k + ahead + 1 - UNROLL))
                for j, b in enumerate(batches):
                    sp.dma_start(x_in[j * TOK:(j + 1) * TOK, slot, :], rows_in[bass.ds(b * TOK, TOK), :]).then_inc(x_loaded[slot], 16)

            def store_y(base, k, back, last=False):
                g = base + (k - back)
                half = (k - back) % 2
                batches = batches_of(g, "stored_batch")
                if last:
                    sp.wait_ge(last_res_ready, 1)
                else:
                    sp.wait_ge(res_ready, g + 1)
                for j, b in enumerate(batches):
                    sp.dma_start(rows_out[bass.ds(b * TOK, TOK), :], y[j * TOK:(j + 1) * TOK, half, :]).then_inc(y_stored[half], 16)

            sp.wait_ge(w_in[0], 16 * len(w_parts(0)))
            load_scales(1)
            sp.dma_start(b_nat[:, :], lora_b.rearrange("i r d -> (i r) d")).then_inc(b_in, 16)
            load_scales(2)
            sp.wait_ge(order_ready, 1)
            for k in range(UNROLL - 1):
                load_x(0, 0, k)
                if k == 0:
                    for n in range(3, 2 * NC):
                        load_scales(n)
            sp.dma_start(down_scale[:, :], down_s.rearrange("d o -> o d").to_broadcast([P, D])).then_inc(down_scale_in, 16)

            def fill_slots():
                sp.wait_ge(ag_hi_ready, 2 * NC)
                sp.wait_ge(ag_lo_ready, 2 * NC)
                for s in range(1, SLOTS):
                    for half in range(HALVES):
                        src = (half * SLOTS + s) * R
                        for term in range(TERMS):
                            dst = (half * TERMS + term) * R
                            part = ag_hi if term // 2 == 0 else ag_lo
                            sp.dma_start(ag_all[dst:dst + R, s * AGW:(s + 1) * AGW].bitcast(F32),
                                         part[src:src + R, :].bitcast(F32)).then_inc(slots_in, 16)

            def group(base, steps, k):
                first = isinstance(base, int) and base + k == 0
                if not first:
                    store_y(base, k, 1)
                if not (isinstance(base, int) and base + k + UNROLL - 1 >= NG):
                    load_x(base, k, UNROLL - 1)
                if first:
                    fill_slots()

            over_groups(sp, group)
            store_y(NG - UNROLL, UNROLL - 1, 0, last=True)
            for half in range(2):
                sp.wait_ge(y_stored[half], 16 * PER * NG // 2)

        @block.gpsimd
        def _(pool):
            for n in range(NW):
                if n >= NBF:
                    pool.wait_ge(wt_ready, WT_END[n - NBF])
                if n < 2 * NC:
                    src = gate_w if n % 2 == 0 else up_w
                    f0 = CHUNKS[n // 2][0]
                    for rows, c0, cols in w_parts(n):
                        r0, tiles = f0 + c0 // D * P, cols // D
                        pool.dma_start(w_bf[0:rows, n % NBF, c0:c0 + cols].rearrange("p (t d) -> p t d", t=tiles),
                                       src[r0:r0 + rows * tiles, :].rearrange("(t p) d -> p t d", t=tiles)).then_inc(w_in[n], 16)
                else:
                    r0 = (n - 2 * NC) * P
                    pool.dma_start(w_bf[:, n % NBF, 0:F], down_w[r0:r0 + P, :]).then_inc(w_in[n], 16)
            def part_slots(base, k, ahead):
                g, par = base + (k + ahead), (k + ahead) % 2
                mask = slot_mask[:, :, bass.ds(g * PER, PER)].unsqueeze(3).to_broadcast([P, SLOTS, PER, TOK])
                pool.wait_ge(w_copied, g + 1)
                nc.gpsimd.tensor_tensor(w_slot[:, par, :, :].rearrange("p s (j t) -> p s j t", j=PER),
                                        w[:, par, :].rearrange("p (j t) -> p j t", j=PER).unsqueeze(1)
                                        .to_broadcast([P, SLOTS, PER, TOK]), mask, ALU.mult).then_inc(parts_ready, 1)

            def add_residual(base, k, back):
                half, slot = (k - back) % 2, (k - back) % UNROLL
                pool.wait_ge(y_scaled, base + (k - back + 1))
                nc.gpsimd.tensor_tensor(y[:, half, :], y[:, half, :], x_in[:, slot, :], ALU.add).then_inc(res_ready, 1)

            pool.wait_ge(order_ready, 2)
            part_slots(0, 0, 0)

            def group(base, steps, k):
                if not (isinstance(base, int) and base + k + 1 == NG):
                    part_slots(base, k, 1)
                if not (isinstance(base, int) and base + k == 0):
                    add_residual(base, k, 1)

            over_groups(pool, group)

        def wt_copy(engine_no, engine, copy, m):
            n, q = WT[m]
            engine.wait_ge(wt_ready, m + 1)
            src = wt_ps[m % WT_RING]
            if n < 2 * NC:
                width = CHUNKS[n // 2][1]
                if n >= 2:
                    engine.wait_ge(ag_ready, n - 1)
                copy(gt[:, n % 2, q, 0:width], src[:, 0:width]).then_inc(wt_copied[engine_no], 1)
            else:
                c = n - 2 * NC
                tiles = blocks_of(CHUNKS[q][1])
                full = sum(size == P for _, size in tiles)
                k0 = CHUNKS[q][0] // P
                last = copy(down_t[:, k0:k0 + full, c * P:(c + 1) * P],
                            src[:, 0:full * P].rearrange("p (t d) -> p t d", t=full))
                if full < len(tiles):
                    size = tiles[-1][1]
                    last = copy(down_t[0:size, k0 + full, c * P:(c + 1) * P], src[0:size, full * P:(full + 1) * P])
                last.then_inc(wt_copied[engine_no], 1)

        def sel_copy(engine_no, engine, copy, n):
            engine.wait_ge(sel_ready, n + 1)
            width = CHUNKS[n // 2][1]
            copy(ag_all[:, ag_columns(n)], sel_ps[n % 2][:, 0:width]).then_inc(sel_copied[engine_no], 1)

        def last_sel_copy(engine_no, engine, copy):
            if SEL_DEAL[2 * NC - 1] == engine_no:
                sel_copy(engine_no, engine, copy, 2 * NC - 1)

        def prepare(engine_no, engine, copy, ag_stage, ag_low, front):
            for n in ROUNDS:
                early, late = ([m for m in part if dealt(m) == engine_no] for part in WT_ROUND[n])
                for m in early:
                    wt_copy(engine_no, engine, copy, m)
                front(n)
                if engine_no == 0:
                    ag_stage(n)
                for m in late:
                    wt_copy(engine_no, engine, copy, m)
                if engine_no == 1:
                    ag_stage(n)
                if n >= 1:
                    if SEL_DEAL[n - 1] == engine_no:
                        sel_copy(engine_no, engine, copy, n - 1)
                ag_low(n)

        @block.scalar
        def _(act):
            def copy(dst, src):
                return nc.scalar.activation(dst, src, ACT.Copy)

            act.wait_ge(sort_consts_in, 16)
            nc.scalar.activation(silu[:, 0, 0:1], kb[:, IDENT * P:IDENT * P + 1], ACT.Silu).then_inc(table_in, 1)
            act.wait_ge(table_in, 1)

            def ag_stage(n):
                if 0 <= n < 2 * NC:
                    width = CHUNKS[n // 2][1]
                    act.wait_ge(ag_scaled, n + 1)
                    copy(ag_hi[:, ag_columns(n)], ag[:, n % 2, 0:width]).then_inc(ag_hi_ready, 1)

            def copy_xt(g):
                act.wait_ge(xt_ready, g + 1)
                reached(act, u_ready, g)
                copy(xt[:, :], xt_ps[:, :]).then_inc(xt_copied, 1)

            def copy_w(g, par):
                act.wait_ge(w_ready, g + 1)
                reached(act, gu_ready, NC * (g - 1))
                reached(act, parts_ready, g - 1)
                copy(w[:, par, :], w_ps).then_inc(w_copied, 1)

            def front(n):
                if n == FRONT - 1:
                    act.wait_ge(bt_ready, 1)
                    copy(bt[:, :, :].rearrange("p c m -> p (c m)"), bank[6][:, :]).then_inc(bt_copied, 1)
                elif n == FRONT:
                    copy_xt(0)
                elif n == FRONT + 2:
                    copy_w(0, 0)

            prepare(1, act, copy, ag_stage, lambda n: None, front)

            def split_hi(s, par):
                act.wait_ge(ht_ready, s + 1)
                reached(act, down_done, s - 1)
                copy(h_hi[:, par, :], ht_ps[:, :]).then_inc(hi_ready, 1)

            def group(base, steps, k):
                g = base + k
                final = isinstance(base, int) and g + 1 == NG
                for c in range(NC):
                    s, par = steps + (k * NC + c), (NC * k + c) % 2
                    if isinstance(s, int) and s == 0:
                        last_sel_copy(1, act, copy)
                    if c == 0 and not final:
                        copy_xt(g + 1)
                    if c == 2 and not final:
                        copy_w(g + 1, (k + 1) % 2)
                    width = CHUNKS[c][1]
                    act.wait_ge(gu_ready, s + 1)
                    reached(act, h_ready, s - 1)
                    nc.scalar.activation(silu[:, par, 0:width], gate_ps[par][:, 0:width], ACT.Silu).then_inc(silu_ready, 1)
                    if not (isinstance(s, int) and s == 0):
                        split_hi(s - 1, 1 - par)

            over_groups(act, group)
            split_hi(NG * NC - 1, (NG * NC - 1) % 2)

        @block.vector
        def _(dve):
            steps = [0]

            def then(instruction):
                steps[0] += 1
                instruction.then_inc(sort_step, 1)
                dve.wait_ge(sort_step, steps[0])

            nc.vector.memset(warm[:, :], 0.0).then_inc(warm_ready, 1)

            dve.wait_ge(ids_in, 32)
            then(nc.vector.tensor_scalar(slot_row[:, :], ids_row[:, :], SLOTS - 1, None, ALU.bitwise_and))
            then(nc.vector.tensor_scalar(slot_col[:, :], ids_col[:, :], SLOTS - 1, None, ALU.bitwise_and))
            dve.wait_ge(sort_consts_in, 16)
            then(nc.vector.tensor_copy(kf[:, :], kb[:, 0:WHI * P]))
            then(nc.vector.scalar_tensor_tensor(key_row[:, :], slot_row[:, :], float(NB), iota, ALU.mult, ALU.add))
            then(nc.vector.scalar_tensor_tensor(key_col[:, :], slot_col[:, :], float(NB), batch_no[:, 0:1], ALU.mult, ALU.add))
            then(nc.vector.tensor_copy(ids_f[:, :], ids_col[:, :]))
            then(nc.vector.tensor_scalar(before[:, :], key_row[:, :], key_col[:, 0:1], None, ALU.is_lt))
            then(nc.vector.tensor_reduce(place[:, :], before[:, :], AX.X, ALU.add))
            nc.vector.tensor_scalar(ids_wide[:, :], iota, 0.0, ids_f[:, 0:1], ALU.mult, ALU.add)
            nc.vector.tensor_scalar(permute[:, :], iota, place[:, 0:1], None, ALU.is_equal).then_inc(permute_ready, 1)

            dve.wait_ge(a_in, 16)
            a_by_chunk = a_f[:, :, :].rearrange("p i (c r) -> p c i r", c=DC)
            hi, lo = (a[:, :, :].rearrange("p c (i r) -> p c i r", i=NA) for a in (a_hi, a_lo))
            then(nc.vector.tensor_copy(hi, a_by_chunk))
            nc.vector.tensor_tensor(lo, a_by_chunk, hi, ALU.subtract).then_inc(a_split, 1)

            def take_order():
                dve.wait_ge(sorted_ready, 1)
                nc.vector.tensor_copy(order[:, :], sort_ps[0:1, 0:NB])
                nc.vector.tensor_copy(sorted_ids[:, :], sort_ps[:, NB:2 * NB]).then_inc(order_ready, 1)
                dve.wait_ge(consts_in, 16)
                nc.vector.tensor_copy(kr[:, :], kb[:, WHI * P:NCONST * P]).then_inc(consts_ready, 1)

            def routes_and_masks():
                nc.vector.tensor_scalar(adapter_mask[:, :], sorted_ids[:, :], adapter_of_row, None, ALU.is_equal)
                then(nc.vector.tensor_scalar(slots_wide[:, :], sorted_ids[:, :], SLOTS - 1, None, ALU.bitwise_and))
                by_group = slots_wide[0:1, :].rearrange("o (g j) -> o g j", j=PER)
                nc.vector.tensor_copy(routes[:, :, 0], by_group[:, :, 0])
                nc.vector.tensor_tensor(routes[:, :, 1], by_group[:, :, PER - 1], by_group[:, :, 0], ALU.subtract)
                wide = slots_wide[:, :].rearrange("p (g j) -> p g j", j=PER)
                then(nc.vector.tensor_tensor(slots_past[:, :].rearrange("p (g j) -> p g j", j=PER), wide,
                                             wide[:, :, 0:1].to_broadcast([P, NG, PER]), ALU.subtract))
                for n in range(SLOTS):
                    last = nc.vector.tensor_scalar(slot_mask[:, n, :], slots_past[:, :], float(n), None, ALU.is_equal)
                last.then_inc(order_ready, 1)

            def ag_stage(n):
                if 0 <= n < 2 * NC:
                    dve.wait_ge(scales_in[n], 16)
                    width = CHUNKS[n // 2][1]
                    dve.wait_ge(ag_ready, n + 1)
                    reached(dve, ag_lo_ready, n - 1)
                    nc.vector.tensor_tensor(ag[:, n % 2, 0:width], ag_ps[:, 0:width], scales[:, ag_columns(n)],
                                            ALU.mult).then_inc(ag_scaled, 1)

            def ag_low(n):
                if not 0 <= n < 2 * NC:
                    return
                par, width = n % 2, CHUNKS[n // 2][1]
                dve.wait_ge(ag_hi_ready, n + 1)
                nc.vector.tensor_tensor(ag_lo[:, ag_columns(n)], ag[:, par, 0:width], ag_hi[:, ag_columns(n)],
                                        ALU.subtract).then_inc(ag_lo_ready, 1)

            def split_u(base, k, ahead):
                g = base + (k + ahead)
                mask = adapter_mask[:, bass.ds(g * PER, PER)].unsqueeze(2).to_broadcast([P, PER, TOK])
                src = u_ps.rearrange("p (j t) -> p j t", j=PER)
                dve.wait_ge(u_ready, g + 1)
                reached(dve, u_split, g)
                nc.vector.tensor_tensor(um[:, :].rearrange("p (j t) -> p j t", j=PER), src, mask, ALU.mult).then_inc(um_ready, 1)
                reached(dve, w_ready, g)
                dve.wait_ge(um_ready, g + 1)
                nc.vector.tensor_copy(u_hi[:, :], um[:, :]).then_inc(u_hi_ready, 1)
                dve.wait_ge(u_hi_ready, g + 1)
                nc.vector.tensor_tensor(u_lo[:, :], um[:, :], u_hi[:, :], ALU.subtract).then_inc(u_split, 1)

            def front(n):
                if n == FRONT - 1:
                    dve.wait_ge(order_ready, 1)
                    routes_and_masks()
                elif n == FRONT + 1:
                    split_u(0, 0, 0)

            take_order()
            prepare(0, dve, nc.vector.tensor_copy, ag_stage, ag_low, front)

            dve.wait_ge(down_scale_in, 16)

            def split_lo(s, par):
                dve.wait_ge(hi_ready, s + 1)
                nc.vector.tensor_tensor(h_lo[:, par, :], ht_ps[:, :], h_hi[:, par, :], ALU.subtract).then_inc(lo_ready, 1)

            def scale_y(base, k, back):
                g, half = base + (k - back), (k - back) % 2
                dve.wait_ge(down_done, NC * (g + 1))
                if not isinstance(g, int) or g >= 2:
                    dve.wait_ge(y_stored[half], 8 * PER * (base + (k - back - half)))
                nc.vector.tensor_tensor(y[:, half, :], y_ps[half][:, :], down_scale[:, :], ALU.mult).then_inc(y_scaled, 1)

            def group(base, steps, k):
                g = base + k
                final = isinstance(base, int) and g + 1 == NG
                for c in range(NC):
                    s, par = steps + (k * NC + c), (NC * k + c) % 2
                    if isinstance(s, int) and s == 0:
                        last_sel_copy(0, dve, nc.vector.tensor_copy)
                    if c == 1 and not final:
                        split_u(base, k, 1)
                    if c == 2 and not (isinstance(g, int) and g == 0):
                        scale_y(base, k, 1)
                    width = CHUNKS[c][1]
                    dve.wait_ge(silu_ready, s + 1)
                    reached(dve, ht_ready, s - 1)
                    nc.vector.tensor_tensor(h[:, par, 0:width], silu[:, par, 0:width], up_ps[par][:, 0:width],
                                            ALU.mult).then_inc(h_ready, 1)
                    if not (isinstance(s, int) and s == 0):
                        split_lo(s - 1, 1 - par)

            over_groups(dve, group)
            split_lo(NG * NC - 1, (NG * NC - 1) % 2)
            scale_y(NG - UNROLL, UNROLL - 1, 0)
            half, slot = (NG - 1) % 2, (NG - 1) % UNROLL
            dve.wait_ge(y_scaled, NG)
            nc.vector.tensor_tensor(y[:, half, :], y[:, half, :], x_in[:, slot, :], ALU.add).then_inc(last_res_ready, 1)

        @block.tensor
        def _(pe):
            def sort_products():
                pe.wait_ge(permute_ready, 1)
                nc.tensor.matmul(sort_ps[:, 0:NB], batch_no, permute[:, :], start=True, stop=True)
                nc.tensor.matmul(sort_ps[:, NB:2 * NB], ids_wide[:, :], permute[:, :], start=True, stop=True)\
                  .then_inc(sorted_ready, 1)

            def wt_transposes(m):
                n, q = WT[m]
                if q == 0:
                    pe.wait_ge(w_in[n], 16 * len(w_parts(n)))
                if m >= WT_RING:
                    before = m - WT_RING
                    pe.wait_ge(wt_copied[dealt(before)], copied_by(dealt(before), before + 1))
                dst = wt_ps[m % WT_RING]
                if n < 2 * NC:
                    for t, (o, size) in enumerate(blocks_of(CHUNKS[n // 2][1])):
                        rows = w_bf[0:size, n % NBF, t * D:(t + 1) * D].rearrange("f (p c) -> f c p", c=DC)
                        last = nc.tensor.transpose(dst[:, o:o + size], rows[:, q, :], ident_bf[0:size, 0:size])
                else:
                    for t, (o, size) in enumerate(blocks_of(CHUNKS[q][1])):
                        at = CHUNKS[q][0] + o
                        last = nc.tensor.transpose(dst[0:size, t * P:(t + 1) * P], w_bf[:, n % NBF, at:at + size],
                                                   ident_bf)
                last.then_inc(wt_ready, 1)

            def ag_products(n):
                if n == 0:
                    pe.wait_ge(a_split, 1)
                width = CHUNKS[n // 2][1]
                reached(pe, ag_scaled, n)
                for e in range(2):
                    pe.wait_ge(wt_copied[e], copied_by(e, WT_END[n]))
                for q in range(DC):
                    for part in (a_lo, a_hi):
                        last = nc.tensor.matmul(ag_ps[:, 0:width], part[:, q, :], gt[:, n % 2, q, 0:width],
                                                start=(q == 0 and part is a_lo), stop=(q == DC - 1 and part is a_hi))
                last.then_inc(ag_ready, 1)

            def spread(n):
                width = CHUNKS[n // 2][1]
                if n == 0:
                    pe.wait_ge(consts_ready, 1)
                pe.wait_ge(ag_lo_ready, n + 1)
                if n == 0:
                    pe.wait_ge(order_ready, 1)
                if n >= 2:
                    pe.wait_ge(sel_copied[SEL_DEAL[n - 2]], sel_copied_by(SEL_DEAL[n - 2], n - 1))
                dst = sel_ps[n % 2][:, 0:width]
                nc.tensor.matmul(dst, selector(SELHI), ag_hi[:, ag_columns(n)], start=True, stop=False)
                nc.tensor.matmul(dst, selector(SELLO), ag_lo[:, ag_columns(n)], start=False, stop=True).then_inc(sel_ready, 1)

            def transpose_x(base, k, ahead):
                g, slot = base + (k + ahead), (k + ahead) % UNROLL
                pe.wait_ge(x_loaded[slot], 16 * (base + (k + ahead - slot)) + 16 * PER)
                for c in range(DC):
                    last = nc.tensor.transpose(xt_ps[:, c * P:(c + 1) * P], x_in[:, slot, c * P:(c + 1) * P], ident)
                last.then_inc(xt_ready, 1)

            def down_ranks(g):
                pe.wait_ge(xt_copied, g + 1)
                for c in range(DC):
                    last = nc.tensor.matmul(u_ps, bt[:, c, :], xt[:, c * P:(c + 1) * P], start=(c == 0), stop=(c == DC - 1))
                last.then_inc(u_ready, 1)

            def spread_u(g):
                if isinstance(g, int) and g == 0:
                    pe.wait_ge(consts_ready, 1)
                pe.wait_ge(u_split, g + 1)
                nc.tensor.matmul(w_ps, selector(WHI), u_hi[:, :], start=True, stop=False)
                nc.tensor.matmul(w_ps, selector(WLO), u_lo[:, :], start=False, stop=True).then_inc(w_ready, 1)

            routes_held = [[pe.alloc_register(f"route{par}{n}") for n in range(2)] for par in range(2)]

            def load_route(g, par):
                pe.load(routes_held[par], routes[0:1, bass.ds(g, 1), :])

            def front(n):
                if n == FRONT - 1:
                    pe.wait_ge(b_in, 16)
                    for c in range(DC):
                        last = nc.tensor.transpose(bank[6][:, c * P:(c + 1) * P], b_nat[:, c * P:(c + 1) * P], ident)
                    last.then_inc(bt_ready, 1)
                elif n == FRONT:
                    pe.wait_ge(bt_copied, 1)
                    transpose_x(0, 0, 0)
                elif n == FRONT + 1:
                    down_ranks(0)
                elif n == FRONT + 2:
                    spread_u(0)
                    load_route(0, 0)

            pe.wait_ge(warm_ready, 1)
            for _ in range(WARMUP):
                nc.tensor.matmul(ag_ps[:, :], warm[:, 0:P], warm[:, :], start=True, stop=True)

            pe.wait_ge(sort_consts_in, 16)
            for n in ROUNDS:
                for m in WT_ROUND[n][0]:
                    wt_transposes(m)
                front(n)
                if n == -1:
                    sort_products()
                if 0 <= n < 2 * NC:
                    ag_products(n)
                for m in WT_ROUND[n][1]:
                    wt_transposes(m)
                if n >= 1:
                    spread(n - 1)

            def spread_in_place(c):
                for e in range(2):
                    pe.wait_ge(sel_copied[e], sel_copied_by(e, 2 * (c + 1)))
                    pe.wait_ge(wt_copied[e], copied_by(e, len(WT) - 2 if c == 0 else len(WT)))

            def gate_up(base, s, k, c, route):
                g, par = base + k, (NC * k + c) % 2
                f0, width = CHUNKS[c]
                first_slot, meets = route

                def products(lhs, slot, start, stop):
                    for kind, dst in ((0, gate_ps[par]), (1, up_ps[par])):
                        at = slot * AGW + (kind * F + f0)
                        last = nc.tensor.matmul(dst[:, 0:width], lhs, ag_all[:, bass.ds(at, width)], start=start, stop=stop)
                    if stop:
                        last.then_inc(gu_ready, 1)

                with pe.If(meets == 0):
                    if c == 0:
                        pe.wait_ge(w_copied, g + 1)
                    products(w[:, k % 2, :], first_slot, True, True)
                with pe.Else():
                    if c == 0:
                        pe.wait_ge(parts_ready, g + 1)
                    with pe.If(meets == 1):
                        for n in range(2):
                            products(w_slot[:, k % 2, n, :], (first_slot + n) % SLOTS, n == 0, n == 1)
                    with pe.Else():
                        for n in range(SLOTS):
                            products(w_slot[:, k % 2, n, :], (first_slot + n) % SLOTS, n == 0, n == SLOTS - 1)

            def transpose_h(s, par, c):
                pe.wait_ge(h_ready, s + 1)
                reached(pe, lo_ready, s)
                for o, size in blocks_of(CHUNKS[c][1]):
                    last = nc.tensor.transpose(ht_ps[0:size, o:o + P], h[:, par, o:o + size], ident)
                last.then_inc(ht_ready, 1)

            def down(g, half, s, par, c):
                if c == 0:
                    reached(pe, y_scaled, g - 1)
                tiles = blocks_of(CHUNKS[c][1])
                for o, size in tiles:
                    n = (CHUNKS[c][0] + o) // P
                    for part in (h_lo, h_hi):
                        last = nc.tensor.matmul(y_ps[half][:, :], part[0:size, par, o:o + P], down_t[0:size, n, :],
                                                start=(n == 0 and part is h_lo),
                                                stop=(c == NC - 1 and o == tiles[-1][0] and part is h_hi))
                last.then_inc(down_done, 1)

            def group(base, steps, k):
                g = base + k
                final = isinstance(base, int) and g + 1 == NG
                first = isinstance(base, int) and g == 0
                route = [pe.snap(r, min_val=0, max_val=SLOTS - 1) for r in routes_held[k % 2]]
                if isinstance(base, int) and g < UNROLL - 1:
                    with pe.If(route[0] + route[1] > 0):
                        pe.wait_ge(slots_in, 16 * SLOT_DMAS)
                elif isinstance(base, int) and g == UNROLL - 1:
                    pe.wait_ge(slots_in, 16 * SLOT_DMAS)
                for c in range(NC):
                    s, par = steps + (k * NC + c), (NC * k + c) % 2
                    if c == 1 and not final:
                        down_ranks(g + 1)
                    if c == 2 and not final:
                        spread_u(g + 1)
                    if first:
                        spread_in_place(c)
                    gate_up(base, s, k, c, route)
                    if c == 0 and not final:
                        transpose_x(base, k, 1)
                    if first and c == 0:
                        spread(2 * NC - 1)
                    if c == 1 and not final:
                        load_route(g + 1, (k + 1) % 2)
                    if not (first and c == 0):
                        transpose_h(s - 1, 1 - par, (c - 1) % NC)
                    if not (first and c < 2):
                        down(g if c == 2 else g - 1, (k + (c == 2) + 1) % 2, s - 2, par, (c - 2) % NC)

            over_groups(pe, group)
            S = NG * NC
            transpose_h(S - 1, (S - 1) % 2, NC - 1)
            down(NG - 1, (NG - 1) % 2, S - 2, S % 2, NC - 2)
            pe.wait_ge(lo_ready, S)
            down(NG - 1, (NG - 1) % 2, S - 1, (S - 1) % 2, NC - 1)


def kernel(x, itok_B_3_7, L0_cond_A, L0_cond_B, L0_ffn_gate_w, L0_ffn_gate_s, L0_ffn_up_w, L0_ffn_up_s,
           L0_ffn_down_w, L0_ffn_down_s):
    import concourse.bacc as bacc
    from concourse.bass_utils import run_bass_kernel_spmd

    arrays = {"x_in_dram": x, "ids_dram": itok_B_3_7, "lora_a_dram": L0_cond_A, "lora_b_dram": L0_cond_B,
              "gate_w_dram": L0_ffn_gate_w, "gate_s_dram": L0_ffn_gate_s, "up_w_dram": L0_ffn_up_w,
              "up_s_dram": L0_ffn_up_s, "down_w_dram": L0_ffn_down_w, "down_s_dram": L0_ffn_down_s,
              "consts_dram": constants()}
    arrays = {name: np.ascontiguousarray(a) for name, a in arrays.items()}
    nc = bacc.Bacc("TRN2", target_bir_lowering=False, num_devices=1)
    aps = [nc.dram_tensor(name, a.shape, mybir.dt.from_np(a.dtype), kind="ExternalInput").ap() for name, a in arrays.items()]
    out = nc.dram_tensor("out_dram", (NB, TOK, D), F32, kind="ExternalOutput").ap()
    program(nc, *aps, out)
    r = run_bass_kernel_spmd(nc, [arrays], core_ids=[0])
    return r.results[0]["out_dram"]
```

```python
from contextlib import ExitStack

import numpy as np

import concourse.bass as bass
from concourse import mybir

F32 = mybir.dt.float32
F32R = mybir.dt.float32r
BF16 = mybir.dt.bfloat16
I32 = mybir.dt.int32
ALU = mybir.AluOpType
ACT = mybir.ActivationFunctionType
AX = mybir.AxisListType

P = 128
NB, TOK, D = 128, 32, 512
NA, R = 8, 16
F = 1376
HALVES, SLOTS = 2, 4
TERMS = 4
PER = 8
NG = NB // PER
GT = PER * TOK
TILES = GT // P
TB = P // TOK
DC = D // P
CW = 512
CHUNKS = [(c, min(CW, F - c)) for c in range(0, F, CW)]
NC = len(CHUNKS)
BLOCKS = [(f, min(P, F - f)) for f in range(0, F, P)]
SB = CW // GT
NS = -(-len(BLOCKS) // SB)
AGW = 2 * F
WARMUP = 10
UNROLL = 4
IOTA, BNUM, IDENT, ADAPTER, WHI, WLO, SELHI, SELLO = 0, 1, 2, 3, 4, 5, 6, 7
NCONST = SELLO + 1
NSEL = NCONST - WHI


def blocks_of(width):
    return [(o, min(P, width - o)) for o in range(0, width, P)]


def constants():
    k = np.zeros((P, NCONST * P), np.float32)

    def put(n, m):
        k[:, n * P:(n + 1) * P] = m

    put(IDENT, np.eye(P))
    src = np.arange(P)
    half, slot, rank = src // (SLOTS * R), src // R % SLOTS, src % R
    dst = np.arange(P)
    dhalf, term, drank = dst // (TERMS * R), dst // R % TERMS, dst % R
    same = (half[:, None] == dhalf) & (rank[:, None] == drank)
    put(WHI, same & (term % 2 == 0))
    put(WLO, same & (term % 2 == 1))
    put(SELHI, same & (slot[:, None] == 0) & (term // 2 == 0))
    put(SELLO, same & (slot[:, None] == 0) & (term // 2 == 1))
    put(IOTA, np.arange(P)[None, :])
    put(BNUM, np.arange(P)[:, None])
    put(ADAPTER, (src // R)[:, None])
    return k.astype(mybir.dt.np(BF16))


def reached(engine, sem, count):
    if not isinstance(count, int) or count > 0:
        engine.wait_ge(sem, count)


def over_groups(engine, group):
    for k in range(UNROLL):
        group(0, 0, k)
    with engine.Fori(1, NG // UNROLL - 1) as turn:
        base = engine.snap(turn * UNROLL)
        steps = engine.snap(turn * (UNROLL * NS))
        for k in range(UNROLL):
            group(base, steps, k)
    for k in range(UNROLL):
        group(NG - UNROLL, (NG - UNROLL) * NS, k)


def program(nc, x, ids, lora_a, lora_b, gate_w, gate_s, up_w, up_s, down_w, down_s, consts, out):
    with ExitStack() as ctx:
        def sb(name, shape, dt):
            return ctx.enter_context(nc.sbuf_tensor(name, shape, dt))

        def sem(name):
            return ctx.enter_context(nc.semaphore(name))

        kb = sb("consts_bf", [P, NCONST * P], BF16)
        kf = sb("consts_f32", [P, WHI * P], F32)
        kr = sb("selectors", [P, NSEL * P], F32R)
        ident_bf = kb[:, IDENT * P:(IDENT + 1) * P]
        iota = kf[:, IOTA * P:(IOTA + 1) * P]
        batch_no = kf[:, BNUM * P:(BNUM + 1) * P]
        ident = kf[:, IDENT * P:(IDENT + 1) * P]
        adapter_of_row = kf[:, ADAPTER * P:ADAPTER * P + 1]

        def selector(n):
            return kr[:, (n - WHI) * P:(n - WHI + 1) * P]

        ids_col = sb("ids_col", [P, 1], I32)
        ids_row = sb("ids_row", [P, NB], I32)
        slot_col = sb("slot_col", [P, 1], I32)
        slot_row = sb("slot_row", [P, NB], I32)
        key_col = sb("key_col", [P, 1], F32)
        key_row = sb("key_row", [P, NB], F32)
        before = sb("before", [P, NB], F32)
        place = sb("place", [P, 1], F32)
        ids_f = sb("ids_f", [P, 1], F32)
        permute = sb("permute", [P, NB], F32)
        ids_wide = sb("ids_wide", [P, P], F32)
        order = sb("order", [1, NB], I32)
        sorted_ids = sb("sorted_ids", [P, NB], I32)
        routes = sb("routes", [1, NG, 2], I32)
        slots_wide = sb("slots_wide", [P, NB], I32)
        slot_mask = sb("slot_mask", [P, SLOTS, NB], F32)
        adapter_mask = sb("adapter_mask", [P, NB], F32)

        a_f = sb("a_f", [P, NA, DC * R], F32)
        a_hi = sb("a_hi", [P, DC, P], F32R)
        a_lo = sb("a_lo", [P, DC, P], F32R)
        b_nat = sb("b_nat", [P, D], F32)
        bt = sb("bt", [P, DC, P], F32)
        down_scale = sb("down_scale", [P, D], F32)
        NBF = 5
        w_bf = sb("w_bf", [P, NBF, 4 * D], BF16)
        gt = sb("gt", [P, 2, DC, CW], F32R)
        ag_hi = sb("ag_hi", [P, AGW], F32R)
        ag_lo = sb("ag_lo", [P, AGW], F32R)
        ag_all = sb("ag_all", [P, SLOTS * AGW], F32R)
        down_t = sb("down_t", [P, len(blocks_of(F)), D], F32R)

        ag_cur = [ag_hi, ag_lo]
        x_in = sb("x_in", [P, UNROLL * TILES, D], F32)
        xt = sb("xt", [P, DC, GT], F32)
        um = sb("um", [P, GT], F32)
        u_hi = sb("u_hi", [P, GT], F32R)
        u_lo = sb("u_lo", [P, GT], F32R)
        w = sb("w", [P, 2, GT], F32R)
        w_slot = sb("w_slot", [P, 2, SLOTS, GT], F32R)
        silu = sb("silu", [P, 2, CW], F32)
        h = sb("h", [P, 2, CW], F32)
        h_hi = sb("h_hi", [P, 2, CW], F32R)
        h_lo = sb("h_lo", [P, 2, CW], F32R)
        Y_RING = 2 * TILES
        y = sb("y", [P, Y_RING, D], F32)
        ag = h
        scales = y

        bank = [ctx.enter_context(nc.psum_tensor(f"bank{n}", [P, CW], F32)) for n in range(8)]
        gate_ps, up_ps = [bank[0], bank[2]], [bank[1], bank[3]]
        y_ps = [bank[4], bank[5]]
        xt_ps, u_ps, w_ps = [bank[6], bank[7]], bank[6][:, 0:GT], bank[7][:, 0:GT]
        wt_ps = [bank[m][:, 0:CW // 2].bitcast(BF16) for m in (0, 1, 2, 4)]
        ag_ps = bank[3]
        sel_ps = [bank[5], bank[7], bank[5], bank[7], bank[5], bank[4]]
        sort_ps = bank[7]
        first_w_ps = bank[6][:, GT:2 * GT]

        warm = sb("warm", [P, CW], BF16)
        warm_ready = sem("warm_ready")
        table_in = sem("table_in")
        sort_consts_in = sem("sort_consts_in")
        consts_in, ids_in, a_in, b_in = sem("consts_in"), sem("ids_in"), sem("a_in"), sem("b_in")
        scales_in, down_scale_in = [sem(f"scales_in{n}") for n in range(2 * NC)], sem("down_scale_in")
        NW = 2 * NC + DC
        w_in = [sem(f"w_in{n}") for n in range(NW)]
        sort_step, consts_ready = sem("sort_step"), sem("consts_ready")
        permute_ready, sorted_ready, order_ready = sem("permute_ready"), sem("sorted_ready"), sem("order_ready")
        bt_ready, bt_copied = sem("bt_ready"), sem("bt_copied")
        a_split = sem("a_split")
        wt_ready, wt_copied = sem("wt_ready"), [sem("wt_copied_dve"), sem("wt_copied_act")]
        ag_ready, ag_scaled, ag_hi_ready, ag_lo_ready = sem("ag_ready"), sem("ag_scaled"), sem("ag_hi_ready"), sem("ag_lo_ready")
        sel_ready, sel_copied = sem("sel_ready"), [sem("sel_copied_dve"), sem("sel_copied_act")]
        slots_in = sem("slots_in")
        x_loaded = [sem(f"x_loaded{k}") for k in range(UNROLL * TILES)]
        ag_in = [sem("ag_in0"), sem("ag_in1")]
        xt_ready, xt_copied = sem("xt_ready"), sem("xt_copied")
        u_ready, um_ready, u_hi_ready, u_split = sem("u_ready"), sem("um_ready"), sem("u_hi_ready"), sem("u_split")
        w_ready, w_copied = sem("w_ready"), sem("w_copied")
        parts_ready = sem("parts_ready")
        gu_ready, silu_ready, h_ready = sem("gu_ready"), sem("silu_ready"), sem("h_ready")
        hi_ready, lo_ready = sem("hi_ready"), sem("lo_ready")
        down_done, y_scaled, res_ready = sem("down_done"), sem("y_scaled"), sem("res_ready")
        last_res_ready = sem("last_res_ready")
        y_stored = [sem(f"y_stored{n}") for n in range(Y_RING)]

        SLOT_DMAS = (SLOTS - 1) * HALVES * TERMS

        def ag_columns(n):
            f0, width = CHUNKS[n // 2]
            return slice(n % 2 * F + f0, n % 2 * F + f0 + width)

        def step_blocks(c):
            return [(b, c * SB + b, BLOCKS[c * SB + b][1]) for b in range(min(SB, len(BLOCKS) - c * SB))]

        def used(buffer, par, c):
            blocks = step_blocks(c)
            return buffer[0:blocks[0][2], par, 0:len(blocks) * GT]

        def used_ps(ps, c):
            blocks = step_blocks(c)
            return ps[0:blocks[0][2], 0:len(blocks) * GT]

        def w_block(n):
            if n < 2 * NC:
                return D, blocks_of(CHUNKS[n // 2][1])
            return F, [(0, P)]

        def w_parts(n):
            width, tiles = w_block(n)
            full = sum(size == P for _, size in tiles)
            parts = [(P, 0, full * width)]
            if full < len(tiles):
                parts.append((tiles[-1][1], full * width, width))
            return parts

        ROUNDS = range(-1, 2 * NC)
        IN_ROUND = {n: [n + 1] for n in range(-1, 2 * NC - 1)} | {2 * NC - 1: []}
        for n in range(DC):
            IN_ROUND[2 * NC - 3 + min(n, 2)].append(2 * NC + n)
        WT_RING = len(wt_ps)
        WT = []
        WT_ROUND, WT_END = {}, {}
        for n in ROUNDS:
            start = len(WT)
            for b in IN_ROUND[n]:
                WT += [(b, q) for q in range(DC if b < 2 * NC else NC)]
                WT_END[b] = len(WT)
            WT_ROUND[n] = range(start, min(start + WT_RING, len(WT))), range(min(start + WT_RING, len(WT)), len(WT))

        DEAL = (1, 1, 1, 1) + (0, 1, 1, 0, 1, 1, 0, 1) * 4

        SEL_DEAL = (0, 1, 0, 1, 1, 0)

        U_STEP, W_STEP = 2, 3

        FRONT = 3

        def dealt(m):
            return DEAL[m]

        def copied_by(engine_no, count):
            return sum(dealt(m) == engine_no for m in range(count))

        def sel_copied_by(engine_no, count):
            return sum(e == engine_no for e in SEL_DEAL[:count])

        block = ctx.enter_context(nc.Block())

        @block.sync
        def _(sp):
            sp.dma_start(ids_row[:, :], ids.rearrange("(o b) -> o b", o=1).to_broadcast([P, NB])).then_inc(ids_in, 16)
            sp.dma_start(ids_col[:, :], ids.rearrange("(b o) -> b o", o=1)).then_inc(ids_in, 16)
            sp.dma_start(kb[:, 0:WHI * P], consts[:, 0:WHI * P]).then_inc(sort_consts_in, 16)

            sp.dma_start(a_f[:, :, :], lora_a.rearrange("i (p c) r -> p i (c r)", c=DC)).then_inc(a_in, 16)
            sp.dma_start(kb[:, WHI * P:NCONST * P], consts[:, WHI * P:NCONST * P]).then_inc(consts_in, 16)

            def load_scales(n):
                (f0, width), src = CHUNKS[n // 2], gate_s if n % 2 == 0 else up_s
                if n >= Y_RING:
                    sp.wait_ge(ag_scaled, n - Y_RING + 1)
                sp.dma_start(scales[:, n % Y_RING, 0:width], src[f0:f0 + width, :].rearrange("f o -> o f").to_broadcast([P, width]))\
                  .then_inc(scales_in[n], 16)

            load_scales(0)

            rows_in = x.rearrange("b n d -> (b n) d")
            rows_out = out.rearrange("b n d -> (b n) d")

            held = {use: [sp.alloc_register(f"{use}{j}") for j in range(TB)] for use in ("loaded_batch", "stored_batch")}
            copied_slot = sp.alloc_register("copied_slot")

            def batches_of(tile, use):
                sp.load(held[use], order[0:1, bass.ds(tile * TB, TB)])
                return [sp.snap(r, min_val=0, max_val=NB - 1) for r in held[use]]

            def load_x(base, k, ahead):
                for t in range(TILES):
                    slot = (k + ahead) % UNROLL * TILES + t
                    tile = (base + (k + ahead)) * TILES + t
                    batches = batches_of(tile, "loaded_batch")
                    if not isinstance(tile, int) or tile >= UNROLL * TILES:
                        sp.wait_ge(res_ready, tile - (UNROLL * TILES - 1))
                    for j, b in enumerate(batches):
                        sp.dma_start(x_in[j * TOK:(j + 1) * TOK, slot, :], rows_in[bass.ds(b * TOK, TOK), :]).then_inc(x_loaded[slot], 16)

            def store_y(base, k, back, tiles=range(TILES), last=False):
                for t in tiles:
                    tile = (base + (k - back)) * TILES + t
                    slot = (k - back) % 2 * TILES + t
                    batches = batches_of(tile, "stored_batch")
                    if last:
                        sp.wait_ge(last_res_ready, t + 1)
                    else:
                        sp.wait_ge(res_ready, tile + 1)
                    for j, b in enumerate(batches):
                        sp.dma_start(rows_out[bass.ds(b * TOK, TOK), :], y[j * TOK:(j + 1) * TOK, slot, :]).then_inc(y_stored[slot], 16)

            sp.wait_ge(w_in[0], 16 * len(w_parts(0)))
            load_scales(1)
            sp.dma_start(b_nat[:, :], lora_b.rearrange("i r d -> (i r) d")).then_inc(b_in, 16)
            load_scales(2)
            sp.wait_ge(order_ready, 1)
            for k in range(UNROLL - 1):
                load_x(0, 0, k)
                if k < 2:
                    load_scales(k + 3)
            load_scales(2 * NC - 1)
            sp.dma_start(down_scale[:, :], down_s.rearrange("d o -> o d").to_broadcast([P, D])).then_inc(down_scale_in, 16)

            def copy_slot(base, steps, k):
                g, par = base + (k + 1), (k + 1) % 2
                sp.load([copied_slot], routes[0:1, bass.ds(g, 1), 0:1])
                slot = sp.snap(copied_slot, min_val=0, max_val=SLOTS - 1)
                sp.wait_ge(gu_ready, steps + k * NS)
                if isinstance(g, int) and g == 2:
                    sp.wait_ge(slots_in, 16 * SLOT_DMAS)
                    sp.wait_ge(sel_ready, 2 * NC)
                sp.dma_start(ag_cur[par][:, :].bitcast(F32), ag_all[:, bass.ds(slot * AGW, AGW)].bitcast(F32)).then_inc(ag_in[par], 16)

            def fill_slots():
                sp.wait_ge(ag_hi_ready, 2 * NC)
                sp.wait_ge(ag_lo_ready, 2 * NC)
                for s in range(1, SLOTS):
                    for half in range(HALVES):
                        src = (half * SLOTS + s) * R
                        for term in range(TERMS):
                            dst = (half * TERMS + term) * R
                            part = ag_hi if term // 2 == 0 else ag_lo
                            sp.dma_start(ag_all[dst:dst + R, s * AGW:(s + 1) * AGW].bitcast(F32),
                                         part[src:src + R, :].bitcast(F32)).then_inc(slots_in, 16)

            def group(base, steps, k):
                first = isinstance(base, int) and base + k == 0
                if not first and not (isinstance(base, int) and base + k + 1 >= NG):
                    copy_slot(base, steps, k)
                if not first:
                    store_y(base, k, 1)
                if not (isinstance(base, int) and base + k + UNROLL - 1 >= NG):
                    load_x(base, k, UNROLL - 1)
                if first:
                    fill_slots()

            over_groups(sp, group)
            store_y(NG - UNROLL, UNROLL - 1, 0, range(TILES - 1), last=True)
            for slot in range(Y_RING):
                sp.wait_ge(y_stored[slot], 16 * TB * NG // 2)

        @block.gpsimd
        def _(pool):
            for n in range(NW):
                if n >= NBF:
                    pool.wait_ge(wt_ready, WT_END[n - NBF])
                if n < 2 * NC:
                    src = gate_w if n % 2 == 0 else up_w
                    f0 = CHUNKS[n // 2][0]
                    for rows, c0, cols in w_parts(n):
                        r0, tiles = f0 + c0 // D * P, cols // D
                        pool.dma_start(w_bf[0:rows, n % NBF, c0:c0 + cols].rearrange("p (t d) -> p t d", t=tiles),
                                       src[r0:r0 + rows * tiles, :].rearrange("(t p) d -> p t d", t=tiles)).then_inc(w_in[n], 16)
                else:
                    r0 = (n - 2 * NC) * P
                    pool.dma_start(w_bf[:, n % NBF, 0:F], down_w[r0:r0 + P, :]).then_inc(w_in[n], 16)

            def part_slots(base, k, ahead):
                g, par = base + (k + ahead), (k + ahead) % 2
                mask = slot_mask[:, :, bass.ds(g * PER, PER)].unsqueeze(3).to_broadcast([P, SLOTS, PER, TOK])
                pool.wait_ge(w_copied, g + 1)
                nc.gpsimd.tensor_tensor(w_slot[:, par, :, :].rearrange("p s (j t) -> p s j t", j=PER),
                                        w[:, par, :].rearrange("p (j t) -> p j t", j=PER).unsqueeze(1)
                                        .to_broadcast([P, SLOTS, PER, TOK]), mask, ALU.mult).then_inc(parts_ready, 1)

            def add_residual(base, k, back):
                for t in range(TILES):
                    slot, x_slot = (k - back) % 2 * TILES + t, (k - back) % UNROLL * TILES + t
                    pool.wait_ge(y_scaled, (base + (k - back)) * TILES + (t + 1))
                    nc.gpsimd.tensor_tensor(y[:, slot, :], y[:, slot, :], x_in[:, x_slot, :], ALU.add).then_inc(res_ready, 1)

            pool.wait_ge(order_ready, 2)
            part_slots(0, 0, 0)

            def group(base, steps, k):
                if not (isinstance(base, int) and base + k == 0):
                    add_residual(base, k, 1)
                if not (isinstance(base, int) and base + k + 1 == NG):
                    part_slots(base, k, 1)

            over_groups(pool, group)

        def wt_copy(engine_no, engine, copy, m):
            n, q = WT[m]
            engine.wait_ge(wt_ready, m + 1)
            src = wt_ps[m % WT_RING]
            if n < 2 * NC:
                width = CHUNKS[n // 2][1]
                if n >= 2:
                    engine.wait_ge(ag_ready, n - 1)
                copy(gt[:, n % 2, q, 0:width], src[:, 0:width]).then_inc(wt_copied[engine_no], 1)
            else:
                c = n - 2 * NC
                tiles = blocks_of(CHUNKS[q][1])
                full = sum(size == P for _, size in tiles)
                k0 = CHUNKS[q][0] // P
                last = copy(down_t[:, k0:k0 + full, c * P:(c + 1) * P],
                            src[:, 0:full * P].rearrange("p (t d) -> p t d", t=full))
                if full < len(tiles):
                    size = tiles[-1][1]
                    last = copy(down_t[0:size, k0 + full, c * P:(c + 1) * P], src[0:size, full * P:(full + 1) * P])
                last.then_inc(wt_copied[engine_no], 1)

        def sel_copy(engine_no, engine, copy, n):
            engine.wait_ge(sel_ready, n + 1)
            width = CHUNKS[n // 2][1]
            copy(ag_all[:, ag_columns(n)], sel_ps[n][:, 0:width]).then_inc(sel_copied[engine_no], 1)

        def last_sel_copy(engine_no, engine, copy):
            if SEL_DEAL[2 * NC - 1] == engine_no:
                sel_copy(engine_no, engine, copy, 2 * NC - 1)

        def prepare(engine_no, engine, copy, ag_stage, ag_low, front):
            for n in ROUNDS:
                early, late = ([m for m in part if dealt(m) == engine_no] for part in WT_ROUND[n])
                for m in early:
                    wt_copy(engine_no, engine, copy, m)
                front(n)
                if engine_no == 0:
                    ag_stage(n)
                for m in late:
                    wt_copy(engine_no, engine, copy, m)
                if engine_no == 1:
                    ag_stage(n)
                if n >= 1:
                    if SEL_DEAL[n - 1] == engine_no:
                        sel_copy(engine_no, engine, copy, n - 1)
                ag_low(n)

        @block.scalar
        def _(act):
            def copy(dst, src):
                return nc.scalar.activation(dst, src, ACT.Copy)

            act.wait_ge(sort_consts_in, 16)
            nc.scalar.activation(silu[:, 0, 0:1], kb[:, IDENT * P:IDENT * P + 1], ACT.Silu).then_inc(table_in, 1)
            act.wait_ge(table_in, 1)

            def ag_stage(n):
                if n == FRONT:
                    copy_xt(0, 0, 0, 1, bank[6])
                if 0 <= n < 2 * NC:
                    width = CHUNKS[n // 2][1]
                    act.wait_ge(ag_scaled, n + 1)
                    copy(ag_hi[:, ag_columns(n)], ag[:, n % 2, 0:width]).then_inc(ag_hi_ready, 1)

            def copy_xt(base, k, ahead, t, ps):
                g = base + (k + ahead)
                act.wait_ge(xt_ready, g * TILES + (t + 1))
                reached(act, u_ready, g)
                copy(xt[:, :, t * P:(t + 1) * P], ps[:, :].rearrange("p (c m) -> p c m", c=DC)).then_inc(xt_copied, 1)

            def copy_w(base, steps, k, ahead, ps):
                g, par = base + (k + ahead), (k + ahead) % 2
                act.wait_ge(w_ready, g + 1)
                if steps is not None:
                    reached(act, gu_ready, steps + k * NS)
                reached(act, parts_ready, g - 1)
                copy(w[:, par, :], ps).then_inc(w_copied, 1)

            def front(n):
                if n == FRONT - 1:
                    act.wait_ge(bt_ready, 1)
                    copy(bt[:, :, :].rearrange("p c m -> p (c m)"), bank[6][:, :]).then_inc(bt_copied, 1)
                elif n == FRONT:
                    copy_xt(0, 0, 0, 0, bank[6])
                elif n == FRONT + 2:
                    copy_w(0, None, 0, 0, first_w_ps)

            prepare(1, act, copy, ag_stage, lambda n: None, front)

            def split_hi(s, par, c):
                act.wait_ge(h_ready, s + 1)
                reached(act, down_done, (s - 1) * TILES)
                copy(used(h_hi, par, c), used(h, par, c)).then_inc(hi_ready, 1)

            def group(base, steps, k):
                g = base + k
                final = isinstance(base, int) and g + 1 == NG
                for c in range(NS):
                    s, par = steps + (k * NS + c), (NS * k + c) % 2
                    if isinstance(s, int) and s == 1:
                        last_sel_copy(1, act, copy)
                    early = isinstance(s, int) and s == 1
                    if early:
                        copy_xt(base, k, 1, c, xt_ps[c])
                    act.wait_ge(gu_ready, s + 1)
                    reached(act, h_ready, s - 1)
                    nc.scalar.activation(used(silu, par, c), used_ps(gate_ps[par], c), ACT.Silu).then_inc(silu_ready, 1)
                    if c in range(TILES) and not early and not final:
                        copy_xt(base, k, 1, c, xt_ps[c])
                    if c == W_STEP and not final:
                        copy_w(base, steps, k, 1, w_ps)
                    split_hi(s, par, c)

            over_groups(act, group)

            held = [act.alloc_register(f"last_batch{j}") for j in range(TB)]
            act.load(held, order[0:1, NB - TB:NB])
            batches = [act.snap(reg, min_val=0, max_val=NB - 1) for reg in held]
            rows_out = out.rearrange("b n d -> (b n) d")
            act.wait_ge(last_res_ready, TILES)
            for j, b in enumerate(batches):
                act.dma_start(rows_out[bass.ds(b * TOK, TOK), :], y[j * TOK:(j + 1) * TOK, Y_RING - 1, :]).then_inc(y_stored[Y_RING - 1], 16)

        @block.vector
        def _(dve):
            steps = [0]

            def then(instruction):
                steps[0] += 1
                instruction.then_inc(sort_step, 1)
                dve.wait_ge(sort_step, steps[0])

            nc.vector.memset(warm[:, :], 0.0).then_inc(warm_ready, 1)

            dve.wait_ge(ids_in, 32)
            then(nc.vector.tensor_scalar(slot_row[:, :], ids_row[:, :], SLOTS - 1, None, ALU.bitwise_and))
            then(nc.vector.tensor_scalar(slot_col[:, :], ids_col[:, :], SLOTS - 1, None, ALU.bitwise_and))
            dve.wait_ge(sort_consts_in, 16)
            then(nc.vector.tensor_copy(kf[:, :], kb[:, 0:WHI * P]))
            then(nc.vector.scalar_tensor_tensor(key_row[:, :], slot_row[:, :], float(NB), iota, ALU.mult, ALU.add))
            then(nc.vector.scalar_tensor_tensor(key_col[:, :], slot_col[:, :], float(NB), batch_no[:, 0:1], ALU.mult, ALU.add))
            then(nc.vector.tensor_copy(ids_f[:, :], ids_col[:, :]))
            then(nc.vector.tensor_scalar(before[:, :], key_row[:, :], key_col[:, 0:1], None, ALU.is_lt))
            then(nc.vector.tensor_reduce(place[:, :], before[:, :], AX.X, ALU.add))
            nc.vector.tensor_scalar(ids_wide[:, :], iota, 0.0, ids_f[:, 0:1], ALU.mult, ALU.add)
            nc.vector.tensor_scalar(permute[:, :], iota, place[:, 0:1], None, ALU.is_equal).then_inc(permute_ready, 1)

            dve.wait_ge(a_in, 16)
            a_by_chunk = a_f[:, :, :].rearrange("p i (c r) -> p c i r", c=DC)
            hi, lo = (a[:, :, :].rearrange("p c (i r) -> p c i r", i=NA) for a in (a_hi, a_lo))
            then(nc.vector.tensor_copy(hi, a_by_chunk))
            nc.vector.tensor_tensor(lo, a_by_chunk, hi, ALU.subtract).then_inc(a_split, 1)

            def take_order():
                dve.wait_ge(sorted_ready, 1)
                nc.vector.tensor_copy(order[:, :], sort_ps[0:1, 0:NB])
                nc.vector.tensor_copy(sorted_ids[:, :], sort_ps[:, NB:2 * NB]).then_inc(order_ready, 1)
                dve.wait_ge(consts_in, 16)
                nc.vector.tensor_copy(kr[:, :], kb[:, WHI * P:NCONST * P]).then_inc(consts_ready, 1)

            def routes_and_masks():
                nc.vector.tensor_scalar(adapter_mask[:, :], sorted_ids[:, :], adapter_of_row, None, ALU.is_equal)
                then(nc.vector.tensor_scalar(slots_wide[:, :], sorted_ids[:, :], SLOTS - 1, None, ALU.bitwise_and))
                by_group = slots_wide[0:1, :].rearrange("o (g j) -> o g j", j=PER)
                nc.vector.tensor_copy(routes[:, :, 0], by_group[:, :, 0])
                nc.vector.tensor_tensor(routes[:, :, 1], by_group[:, :, PER - 1], by_group[:, :, 0], ALU.subtract)
                for n in range(SLOTS):
                    last = nc.vector.tensor_scalar(slot_mask[:, n, :], slots_wide[:, :], float(n), None, ALU.is_equal)
                last.then_inc(order_ready, 1)

            def ag_stage(n):
                if 0 <= n < 2 * NC:
                    dve.wait_ge(scales_in[n], 16)
                    width = CHUNKS[n // 2][1]
                    dve.wait_ge(ag_ready, n + 1)
                    reached(dve, ag_lo_ready, n - 1)
                    nc.vector.tensor_tensor(ag[:, n % 2, 0:width], ag_ps[:, 0:width], scales[:, n % Y_RING, 0:width],
                                            ALU.mult).then_inc(ag_scaled, 1)

            def ag_low(n):
                if not 0 <= n < 2 * NC:
                    return
                par, width = n % 2, CHUNKS[n // 2][1]
                dve.wait_ge(ag_hi_ready, n + 1)
                nc.vector.tensor_tensor(ag_lo[:, ag_columns(n)], ag[:, par, 0:width], ag_hi[:, ag_columns(n)],
                                        ALU.subtract).then_inc(ag_lo_ready, 1)
                if n == FRONT - 1:
                    dve.wait_ge(order_ready, 1)
                    routes_and_masks()

            def split_u(base, k, ahead):
                g = base + (k + ahead)
                mask = adapter_mask[:, bass.ds(g * PER, PER)].unsqueeze(2).to_broadcast([P, PER, TOK])
                src = u_ps.rearrange("p (j t) -> p j t", j=PER)
                dve.wait_ge(u_ready, g + 1)
                reached(dve, u_split, g)
                nc.vector.tensor_tensor(um[:, :].rearrange("p (j t) -> p j t", j=PER), src, mask, ALU.mult).then_inc(um_ready, 1)
                reached(dve, w_ready, g)
                dve.wait_ge(um_ready, g + 1)
                nc.vector.tensor_copy(u_hi[:, :], um[:, :]).then_inc(u_hi_ready, 1)
                dve.wait_ge(u_hi_ready, g + 1)
                nc.vector.tensor_tensor(u_lo[:, :], um[:, :], u_hi[:, :], ALU.subtract).then_inc(u_split, 1)

            def front(n):
                if n == FRONT + 1:
                    split_u(0, 0, 0)

            take_order()
            prepare(0, dve, nc.vector.tensor_copy, ag_stage, ag_low, front)

            dve.wait_ge(down_scale_in, 16)

            def split_lo(s, par, c):
                dve.wait_ge(hi_ready, s + 1)
                nc.vector.tensor_tensor(used(h_lo, par, c), used(h, par, c), used(h_hi, par, c), ALU.subtract).then_inc(lo_ready, 1)

            def scale_y(base, k, back, tiles=range(TILES)):
                for t in tiles:
                    tile, slot = (base + (k - back)) * TILES + t, (k - back) % 2 * TILES + t
                    if back == 0:
                        dve.wait_ge(down_done, NG * NS * TILES - 2 * (TILES - 1 - t))
                    else:
                        dve.wait_ge(down_done, (base + (k - back)) * (NS * TILES) + ((NS - 1) * TILES + t + 1))
                    if not isinstance(tile, int) or tile >= Y_RING:
                        dve.wait_ge(y_stored[slot], 16 * TB // Y_RING * (tile - slot))
                    nc.vector.tensor_tensor(y[:, slot, :], y_ps[t][:, :], down_scale[:, :], ALU.mult).then_inc(y_scaled, 1)

            def group(base, steps, k):
                g = base + k
                final = isinstance(base, int) and g + 1 == NG
                for c in range(NS):
                    s, par = steps + (k * NS + c), (NS * k + c) % 2
                    if isinstance(s, int) and s == 1:
                        last_sel_copy(0, dve, nc.vector.tensor_copy)
                    dve.wait_ge(silu_ready, s + 1)
                    reached(dve, lo_ready, s - 1)
                    nc.vector.tensor_tensor(used(h, par, c), used(silu, par, c), used_ps(up_ps[par], c), ALU.mult).then_inc(h_ready, 1)
                    if c == 1 and not (isinstance(g, int) and g == 0):
                        scale_y(base, k, 1)
                    if c == U_STEP and not final:
                        split_u(base, k, 1)
                    split_lo(s, par, c)

            over_groups(dve, group)
            for t in range(TILES):
                scale_y(NG - UNROLL, UNROLL - 1, 0, (t,))
                slot, x_slot = (NG - 1) % 2 * TILES + t, (NG - 1) % UNROLL * TILES + t
                dve.wait_ge(y_scaled, (NG - 1) * TILES + t + 1)
                nc.vector.tensor_tensor(y[:, slot, :], y[:, slot, :], x_in[:, x_slot, :], ALU.add).then_inc(last_res_ready, 1)

        @block.tensor
        def _(pe):
            def sort_products():
                pe.wait_ge(permute_ready, 1)
                nc.tensor.matmul(sort_ps[:, 0:NB], batch_no, permute[:, :], start=True, stop=True)
                nc.tensor.matmul(sort_ps[:, NB:2 * NB], ids_wide[:, :], permute[:, :], start=True, stop=True)\
                  .then_inc(sorted_ready, 1)

            def wt_transposes(m):
                n, q = WT[m]
                if q == 0:
                    pe.wait_ge(w_in[n], 16 * len(w_parts(n)))
                if m >= WT_RING:
                    before = m - WT_RING
                    pe.wait_ge(wt_copied[dealt(before)], copied_by(dealt(before), before + 1))
                dst = wt_ps[m % WT_RING]
                if n < 2 * NC:
                    for t, (o, size) in enumerate(blocks_of(CHUNKS[n // 2][1])):
                        rows = w_bf[0:size, n % NBF, t * D:(t + 1) * D].rearrange("f (p c) -> f c p", c=DC)
                        last = nc.tensor.transpose(dst[:, o:o + size], rows[:, q, :], ident_bf[0:size, 0:size])
                else:
                    for t, (o, size) in enumerate(blocks_of(CHUNKS[q][1])):
                        at = CHUNKS[q][0] + o
                        last = nc.tensor.transpose(dst[0:size, t * P:(t + 1) * P], w_bf[:, n % NBF, at:at + size],
                                                   ident_bf)
                last.then_inc(wt_ready, 1)

            def ag_products(n):
                if n == 0:
                    pe.wait_ge(a_split, 1)
                width = CHUNKS[n // 2][1]
                reached(pe, ag_scaled, n)
                for e in range(2):
                    pe.wait_ge(wt_copied[e], copied_by(e, WT_END[n]))
                for q in range(DC):
                    for part in (a_lo, a_hi):
                        last = nc.tensor.matmul(ag_ps[:, 0:width], part[:, q, :], gt[:, n % 2, q, 0:width],
                                                start=(q == 0 and part is a_lo), stop=(q == DC - 1 and part is a_hi))
                last.then_inc(ag_ready, 1)

            def spread(n):
                width = CHUNKS[n // 2][1]
                if n == 0:
                    pe.wait_ge(consts_ready, 1)
                pe.wait_ge(ag_lo_ready, n + 1)
                if n == 0:
                    pe.wait_ge(order_ready, 1)
                if 2 <= n < 2 * NC - 1:
                    pe.wait_ge(sel_copied[SEL_DEAL[n - 2]], sel_copied_by(SEL_DEAL[n - 2], n - 1))
                dst = sel_ps[n][:, 0:width]
                nc.tensor.matmul(dst, selector(SELHI), ag_hi[:, ag_columns(n)], start=True, stop=False)
                nc.tensor.matmul(dst, selector(SELLO), ag_lo[:, ag_columns(n)], start=False, stop=True).then_inc(sel_ready, 1)

            def transpose_x(base, k, ahead, t, ps):
                slot = (k + ahead) % UNROLL * TILES + t
                pe.wait_ge(x_loaded[slot], 16 * TB // UNROLL * (base + (k + ahead) - (k + ahead) % UNROLL) + 16 * TB)
                for c in range(DC):
                    last = nc.tensor.transpose(ps[:, c * P:(c + 1) * P], x_in[:, slot, c * P:(c + 1) * P], ident)
                last.then_inc(xt_ready, 1)

            def down_ranks(g):
                pe.wait_ge(xt_copied, g * TILES + TILES)
                for c in range(DC):
                    last = nc.tensor.matmul(u_ps, bt[:, c, :], xt[:, c, :], start=(c == 0), stop=(c == DC - 1))
                last.then_inc(u_ready, 1)

            def spread_u(g, ps):
                pe.wait_ge(u_split, g + 1)
                nc.tensor.matmul(ps, selector(WHI), u_hi[:, :], start=True, stop=False)
                nc.tensor.matmul(ps, selector(WLO), u_lo[:, :], start=False, stop=True).then_inc(w_ready, 1)

            routes_held = [[pe.alloc_register(f"route{par}{n}") for n in range(2)] for par in range(2)]

            def load_route(g, par):
                pe.load(routes_held[par], routes[0:1, bass.ds(g, 1), :])

            def front(n):
                if n == FRONT - 1:
                    pe.wait_ge(b_in, 16)
                    for c in range(DC):
                        last = nc.tensor.transpose(bank[6][:, c * P:(c + 1) * P], b_nat[:, c * P:(c + 1) * P], ident)
                    last.then_inc(bt_ready, 1)
                elif n == FRONT:
                    pe.wait_ge(bt_copied, 1)
                    transpose_x(0, 0, 0, 0, bank[6])
                elif n == FRONT + 1:
                    down_ranks(0)
                elif n == FRONT + 2:
                    spread_u(0, first_w_ps)
                    load_route(0, 0)

            pe.wait_ge(warm_ready, 1)
            for _ in range(WARMUP):
                nc.tensor.matmul(ag_ps[:, :], warm[:, 0:P], warm[:, :], start=True, stop=True)

            pe.wait_ge(sort_consts_in, 16)
            for n in ROUNDS:
                for m in WT_ROUND[n][0]:
                    wt_transposes(m)
                front(n)
                if n == -1:
                    sort_products()
                if 0 <= n < 2 * NC:
                    ag_products(n)
                for m in WT_ROUND[n][1]:
                    wt_transposes(m)
                if n == FRONT:
                    pe.wait_ge(xt_copied, 1)
                    transpose_x(0, 0, 0, 1, bank[6])
                if n >= 1:
                    spread(n - 1)

            def spread_in_place(c):
                for e in range(2):
                    pe.wait_ge(sel_copied[e], sel_copied_by(e, 2 * (c * SB * P // CW + 1)))
                    pe.wait_ge(wt_copied[e], copied_by(e, len(WT) - 2 if c == 0 else len(WT)))

            def gate_up(base, steps, k, c, route):
                g, s, par = base + k, steps + (k * NS + c), (NS * k + c) % 2
                first_slot, meets = route

                def products(terms):
                    for b, n, size in step_blocks(c):
                        for kind, dst in ((0, gate_ps[par]), (1, up_ps[par])):
                            for m, (ag, at, rhs) in enumerate(terms):
                                col = at + kind * F + BLOCKS[n][0]
                                last = nc.tensor.matmul(dst[0:size, b * GT:(b + 1) * GT], ag[:, col:col + size], rhs,
                                                        start=(m == 0), stop=(m == len(terms) - 1))
                    last.then_inc(gu_ready, 1)

                def slot_copied():
                    pe.wait_ge(ag_in[k % 2], 8 * (base + (k - k % 2)))

                def passes(slots):
                    reached(pe, h_ready, s - 1)
                    if c == 0:
                        pe.wait_ge(parts_ready, g + 1)
                        if not (isinstance(g, int) and g < 2):
                            slot_copied()
                    products([(ag_all, n * AGW, w_slot[:, k % 2, n, :]) for n in slots])

                def one_slot(ag):
                    reached(pe, h_ready, s - 1)
                    if c == 0:
                        pe.wait_ge(w_copied, g + 1)
                        if ag is not ag_all:
                            slot_copied()
                    products([(ag, 0, w[:, k % 2, :])])

                if isinstance(g, int) and g < 2:
                    with pe.If(first_slot + meets == 0):
                        one_slot(ag_all)
                    with pe.Else():
                        if s == 0:
                            pe.wait_ge(slots_in, 16 * SLOT_DMAS)
                        passes(range(SLOTS))
                    return
                with pe.If(meets == 0):
                    one_slot(ag_cur[k % 2])
                with pe.Else():
                    with pe.If(meets == 1):
                        with pe.If(first_slot == 0):
                            passes((0, 1))
                        with pe.Else():
                            with pe.If(first_slot == 1):
                                passes((1, 2))
                            with pe.Else():
                                passes((2, 3))
                    with pe.Else():
                        passes(range(SLOTS))

            def down(g, s, par, c, tiles=range(TILES)):
                pe.wait_ge(lo_ready, s + 1)
                blocks = step_blocks(c)
                for t in tiles:
                    if c == 0:
                        reached(pe, y_scaled, (g - 1) * TILES + (t + 1))
                    for b, n, size in blocks:
                        for part in (h_lo, h_hi):
                            last = nc.tensor.matmul(y_ps[t][:, :], part[0:size, par, b * GT + t * P:b * GT + (t + 1) * P],
                                                    down_t[0:size, n, :], start=(n == 0 and part is h_lo),
                                                    stop=(n == len(BLOCKS) - 1 and part is h_hi))
                    last.then_inc(down_done, 1)

            def group(base, steps, k):
                g = base + k
                final = isinstance(base, int) and g + 1 == NG
                first = isinstance(base, int) and g == 0
                route = [pe.snap(r, min_val=0, max_val=SLOTS - 1) for r in routes_held[k % 2]]
                for c in range(NS):
                    s, par = steps + (k * NS + c), (NS * k + c) % 2
                    if first:
                        spread_in_place(c)
                    gate_up(base, steps, k, c, route)
                    if not final:
                        if first and c == 1:
                            for e in range(2):
                                pe.wait_ge(sel_copied[e], sel_copied_by(e, 2 * NC - 2))
                        if c in range(TILES):
                            transpose_x(base, k, 1, c, xt_ps[c])
                        if c == 1:
                            load_route(g + 1, (k + 1) % 2)
                        if c == U_STEP:
                            down_ranks(g + 1)
                        if c == W_STEP + 0:
                            spread_u(g + 1, w_ps)
                    if first and c == 1:
                        spread(2 * NC - 1)
                    if first and c == 2:
                        for e in range(2):
                            pe.wait_ge(sel_copied[e], sel_copied_by(e, 2 * NC))
                    if not (first and c < 2):
                        down(g if c >= 2 else g - 1, s - 2, par, (c - 2) % NS)

            over_groups(pe, group)
            S = NG * NS
            for t in range(TILES):
                down(NG - 1, S - 2, S % 2, NS - 2, (t,))
                down(NG - 1, S - 1, (S - 1) % 2, NS - 1, (t,))



def kernel(x, itok_B_3_7, L0_cond_A, L0_cond_B, L0_ffn_gate_w, L0_ffn_gate_s, L0_ffn_up_w, L0_ffn_up_s,
           L0_ffn_down_w, L0_ffn_down_s):
    import concourse.bacc as bacc
    from concourse.bass_utils import run_bass_kernel_spmd

    arrays = {"x_in_dram": x, "ids_dram": itok_B_3_7, "lora_a_dram": L0_cond_A, "lora_b_dram": L0_cond_B,
              "gate_w_dram": L0_ffn_gate_w, "gate_s_dram": L0_ffn_gate_s, "up_w_dram": L0_ffn_up_w,
              "up_s_dram": L0_ffn_up_s, "down_w_dram": L0_ffn_down_w, "down_s_dram": L0_ffn_down_s,
              "consts_dram": constants()}
    arrays = {name: np.ascontiguousarray(a) for name, a in arrays.items()}
    nc = bacc.Bacc("TRN2", target_bir_lowering=False, num_devices=1)
    aps = [nc.dram_tensor(name, a.shape, mybir.dt.from_np(a.dtype), kind="ExternalInput").ap() for name, a in arrays.items()]
    out = nc.dram_tensor("out_dram", (NB, TOK, D), F32, kind="ExternalOutput").ap()
    program(nc, *aps, out)
    r = run_bass_kernel_spmd(nc, [arrays], core_ids=[0])
    return r.results[0]["out_dram"]
```
